# Optimizing a Trainium2 kernel written in Bass

```python
import numpy as np
import jax
import jax.numpy as jnp

def _softmax(x, axis=-1):
    return jax.nn.softmax(x, axis=axis)

def _gelu(x):
    return jax.nn.gelu(x, approximate=True)

def _silu(x):
    return jax.nn.silu(x)

def _sigmoid(x):
    return jax.nn.sigmoid(x)

def _layernorm(x, axis=-1, eps=1e-05):
    m = jnp.mean(x, axis=axis, keepdims=True)
    v = jnp.var(x, axis=axis, keepdims=True)
    return (x - m) / jnp.sqrt(v + eps)

def _scatter_add(tgt, idx, src, axis=0):
    return tgt.at[idx].add(src)

def _segment_sum(src, seg, n):
    return jax.ops.segment_sum(src, seg, n)
kernel_name = 'mk_gnn_preln_d1_gnn_r8_1cdf9e'

def setup_inputs(seed: int=0):
    np.random.seed(seed)
    _w = jnp.asarray

    def _rec_inputs():
        import jax
        import jax.numpy as jnp
        _gk = jax.random.key(seed)
        x = -6.985e-05 + 0.9998 * jax.random.normal(jax.random.fold_in(_gk, 1), (1250, 512), jnp.float32)
        src = jax.random.randint(jax.random.fold_in(_gk, 2), (20000,), 0, 1250, jnp.int32)
        dst = jax.random.randint(jax.random.fold_in(_gk, 3), (20000,), 0, 1250, jnp.int32)
        _o = jnp.argsort(dst, stable=True)
        src = src[_o]
        dst = dst[_o]
        return (x, src, dst)
    x, src, dst = _rec_inputs()

    def _L0_gnn_setup():
        import jax, jax.numpy as jnp
        import numpy as np
        B = 32
        MAXN = 256
        HEADS = 8
        DH = 64
        M = 256
        D = 512
        EPS = 1e-05
        KEPS = 1e-06

        def _batchnorm(x, g, b):
            mu = jnp.mean(x, axis=0)
            var = jnp.mean((x - mu) ** 2, axis=0)
            return (x - mu) * jax.lax.rsqrt(var + EPS) * g + b

        def _forward(x, batch, edge_index, norm1_g, norm1_b, norm2_g, norm2_b, W_conv, b_conv, Wq, Wk, Wv, Wo, proj):
            N = x.shape[0]
            E = edge_index.shape[1]
            h = x
            xn = _batchnorm(x, norm1_g, norm1_b)
            msg = xn[edge_index[0]]
            agg = jax.ops.segment_sum(msg, edge_index[1], num_segments=N)
            deg = jax.ops.segment_sum(jnp.ones((E,), x.dtype), edge_index[1], num_segments=N)
            agg = agg / jnp.maximum(deg, 1.0)[:, None]
            conv_out = jax.nn.relu(agg @ W_conv + b_conv)
            counts = jax.ops.segment_sum(jnp.ones((N,), jnp.int32), batch, num_segments=B)
            offsets = jnp.concatenate([jnp.zeros((1,), jnp.int32), jnp.cumsum(counts)[:-1]])
            pos = jnp.arange(N, dtype=jnp.int32) - offsets[batch]
            h_dense = jnp.zeros((B, MAXN, D), x.dtype).at[batch, pos].set(h)
            mask = jnp.zeros((B, MAXN), bool).at[batch, pos].set(True)

            def heads(t, W):
                return (t @ W).reshape(B, MAXN, HEADS, DH).transpose(0, 2, 1, 3)
            q, k, v = (heads(h_dense, Wq), heads(h_dense, Wk), heads(h_dense, Wv))
            scale = DH ** (-0.25)

            def phi(t, is_query):
                t = t * scale
                u = jnp.einsum('bhnd,md->bhnm', t, proj)
                diag = 0.5 * jnp.sum(t * t, axis=-1, keepdims=True)
                if is_query:
                    m_ = jnp.max(u, axis=-1, keepdims=True)
                else:
                    m_ = jnp.max(u, axis=(-2, -1), keepdims=True)
                return jnp.exp(u - diag - jax.lax.stop_gradient(m_)) / np.sqrt(M) + KEPS
            qf = phi(q, True)
            kf = phi(k, False) * mask[:, None, :, None]
            vm = v * mask[:, None, :, None]
            kv = jnp.einsum('bhnm,bhnd->bhmd', kf, vm)
            z = 1.0 / (jnp.einsum('bhnm,bhm->bhn', qf, kf.sum(axis=2)) + KEPS)
            attn = jnp.einsum('bhnm,bhmd->bhnd', qf, kv) * z[..., None]
            attn = attn.transpose(0, 2, 1, 3).reshape(B, MAXN, D) @ Wo
            h_attn = attn[batch, pos]
            return _batchnorm(conv_out + h_attn + h, norm2_g, norm2_b)
        key = jax.random.key(seed)
        ks = jax.random.split(key, 10)
        sizes = 1024 + np.arange(B) * 131 % 1025
        N = int(sizes.sum())
        E = N * 8
        batch = jnp.asarray(np.repeat(np.arange(B), sizes), dtype=jnp.int32)
        edge_index = jax.random.randint(ks[0], (2, E), 0, N, dtype=jnp.int32)
        s = 1.0 / np.sqrt(D)
        return {'x': jax.random.normal(ks[1], (N, D), jnp.float32), 'batch': batch, 'edge_index': edge_index, 'norm1_g': jnp.ones((D,), jnp.float32), 'norm1_b': jnp.zeros((D,), jnp.float32), 'norm2_g': jnp.ones((D,), jnp.float32), 'norm2_b': jnp.zeros((D,), jnp.float32), 'W_conv': jax.random.normal(ks[2], (D, D), jnp.float32) * s, 'b_conv': jnp.zeros((D,), jnp.float32), 'Wq': jax.random.normal(ks[3], (D, D), jnp.float32) * s, 'Wk': jax.random.normal(ks[4], (D, D), jnp.float32) * s, 'Wv': jax.random.normal(ks[5], (D, D), jnp.float32) * s, 'Wo': jax.random.normal(ks[6], (D, D), jnp.float32) * s, 'proj': jax.random.normal(ks[7], (M, DH), jnp.float32)}
    _L0_gnn_all = _L0_gnn_setup()
    _L0_gnn_in = {k: v for k, v in _L0_gnn_all.items() if k in ('norm1_g', 'norm1_b', 'norm2_g', 'norm2_b', 'W_conv', 'b_conv', 'Wq', 'Wk', 'Wv', 'Wo', 'proj')}
    del _L0_gnn_all
    return {'x': x, 'src': src, 'dst': dst, 'L0_gnn_norm1_g': _L0_gnn_in['norm1_g'], 'L0_gnn_norm1_b': _L0_gnn_in['norm1_b'], 'L0_gnn_norm2_g': _L0_gnn_in['norm2_g'], 'L0_gnn_norm2_b': _L0_gnn_in['norm2_b'], 'L0_gnn_W_conv': _L0_gnn_in['W_conv'], 'L0_gnn_b_conv': _L0_gnn_in['b_conv'], 'L0_gnn_Wq': _L0_gnn_in['Wq'], 'L0_gnn_Wk': _L0_gnn_in['Wk'], 'L0_gnn_Wv': _L0_gnn_in['Wv'], 'L0_gnn_Wo': _L0_gnn_in['Wo'], 'L0_gnn_proj': _L0_gnn_in['proj']}

def reference(x, src, dst, L0_gnn_norm1_g, L0_gnn_norm1_b, L0_gnn_norm2_g, L0_gnn_norm2_b, L0_gnn_W_conv, L0_gnn_b_conv, L0_gnn_Wq, L0_gnn_Wk, L0_gnn_Wv, L0_gnn_Wo, L0_gnn_proj):
    import jax
    import jax.numpy as jnp

    def _L0_gnn_ref(x, batch, edge_index, norm1_g, norm1_b, norm2_g, norm2_b, W_conv, b_conv, Wq, Wk, Wv, Wo, proj):
        import jax, jax.numpy as jnp
        import numpy as np
        B = 32
        MAXN = 256
        HEADS = 8
        DH = 64
        M = 256
        D = 512
        EPS = 1e-05
        KEPS = 1e-06

        def _batchnorm(x, g, b):
            mu = jnp.mean(x, axis=0)
            var = jnp.mean((x - mu) ** 2, axis=0)
            return (x - mu) * jax.lax.rsqrt(var + EPS) * g + b

        def _forward(x, batch, edge_index, norm1_g, norm1_b, norm2_g, norm2_b, W_conv, b_conv, Wq, Wk, Wv, Wo, proj):
            N = x.shape[0]
            E = edge_index.shape[1]
            h = x
            xn = _batchnorm(x, norm1_g, norm1_b)
            msg = xn[edge_index[0]]
            agg = jax.ops.segment_sum(msg, edge_index[1], num_segments=N)
            deg = jax.ops.segment_sum(jnp.ones((E,), x.dtype), edge_index[1], num_segments=N)
            agg = agg / jnp.maximum(deg, 1.0)[:, None]
            conv_out = jax.nn.relu(agg @ W_conv + b_conv)
            counts = jax.ops.segment_sum(jnp.ones((N,), jnp.int32), batch, num_segments=B)
            offsets = jnp.concatenate([jnp.zeros((1,), jnp.int32), jnp.cumsum(counts)[:-1]])
            pos = jnp.arange(N, dtype=jnp.int32) - offsets[batch]
            h_dense = jnp.zeros((B, MAXN, D), x.dtype).at[batch, pos].set(h)
            mask = jnp.zeros((B, MAXN), bool).at[batch, pos].set(True)

            def heads(t, W):
                return (t @ W).reshape(B, MAXN, HEADS, DH).transpose(0, 2, 1, 3)
            q, k, v = (heads(h_dense, Wq), heads(h_dense, Wk), heads(h_dense, Wv))
            scale = DH ** (-0.25)

            def phi(t, is_query):
                t = t * scale
                u = jnp.einsum('bhnd,md->bhnm', t, proj)
                diag = 0.5 * jnp.sum(t * t, axis=-1, keepdims=True)
                if is_query:
                    m_ = jnp.max(u, axis=-1, keepdims=True)
                else:
                    m_ = jnp.max(u, axis=(-2, -1), keepdims=True)
                return jnp.exp(u - diag - jax.lax.stop_gradient(m_)) / np.sqrt(M) + KEPS
            qf = phi(q, True)
            kf = phi(k, False) * mask[:, None, :, None]
            vm = v * mask[:, None, :, None]
            kv = jnp.einsum('bhnm,bhnd->bhmd', kf, vm)
            z = 1.0 / (jnp.einsum('bhnm,bhm->bhn', qf, kf.sum(axis=2)) + KEPS)
            attn = jnp.einsum('bhnm,bhmd->bhnd', qf, kv) * z[..., None]
            attn = attn.transpose(0, 2, 1, 3).reshape(B, MAXN, D) @ Wo
            h_attn = attn[batch, pos]
            return _batchnorm(conv_out + h_attn + h, norm2_g, norm2_b)
        return _forward(x, batch, edge_index, norm1_g, norm1_b, norm2_g, norm2_b, W_conv, b_conv, Wq, Wk, Wv, Wo, proj)
    edge_index = jnp.stack([src, dst])
    batch0 = jnp.zeros((1250,), jnp.int32)
    h = jnp.maximum(_layernorm(x, axis=-1), 0.0)
    x = x + _L0_gnn_ref(h, batch0, edge_index, L0_gnn_norm1_g, L0_gnn_norm1_b, L0_gnn_norm2_g, L0_gnn_norm2_b, L0_gnn_W_conv, L0_gnn_b_conv, L0_gnn_Wq, L0_gnn_Wk, L0_gnn_Wv, L0_gnn_Wo, L0_gnn_proj)
    return x

_drawn_inputs = setup_inputs


def setup_inputs(seed=0):
    import zlib

    import numpy as np

    out = dict(_drawn_inputs(seed))
    spreads = {'L0_gnn_norm1_g': (1.0, 0.2),
     'L0_gnn_norm1_b': (0.0, 0.1),
     'L0_gnn_norm2_g': (1.0, 0.2),
     'L0_gnn_norm2_b': (0.0, 0.1),
     'L0_gnn_b_conv': (0.0, 0.1)}
    factors = {'L0_gnn_Wq': 26.728,
     'L0_gnn_Wk': 25.936,
     'L0_gnn_Wv': 26.392,
     'L0_gnn_Wo': 26.768,
     'L0_gnn_proj': 29.208}
    for name, (base, spread) in spreads.items():
        noise = np.random.default_rng([zlib.crc32(name.encode()), seed]).standard_normal(out[name].shape)
        drawn = base * np.exp(spread * noise) if base else spread * noise
        out[name] = jnp.asarray(drawn.astype(out[name].dtype))
    for name, factor in factors.items():
        out[name] = (out[name] * factor).astype(out[name].dtype)
    return out
```

```python
from contextlib import ExitStack

import concourse.bass as bass
from concourse import mybir

ALU = mybir.AluOpType
ACT = mybir.ActivationFunctionType
AX_X = mybir.AxisListType.X
F32 = mybir.dt.float32
F16 = mybir.dt.float16
BF16 = mybir.dt.bfloat16
I32 = mybir.dt.int32
U32 = mybir.dt.uint32
ds = bass.ds

P = 128
N = 1250
D = 512
E = 20000
NT = (N + P - 1) // P
LAST = N - (NT - 1) * P
FT = D // P
HEADS, DH, M = 8, 64, 256
NA = 256
AT = NA // P
EPS, KEPS = 1e-5, 1e-6
QK_SCALE = DH ** -0.25
PHI_SCALE = 1.0 / M ** 0.5

W = 25
NW = N // W
NPAIR = NW // 2
K = 4
CAP = K * P
GR = 16
NSTEP = NW * K
HALF = NSTEP // 2
NROW = E // GR + (K - 1) * P // GR
FULL = (E - P) // GR + 1
TAIL0 = FULL * GR
TAILN = (NROW - FULL - 1) * GR + P
RING = 16
HSCALE = 2048.0
CHUNKS = [(0, 500), (500, 500), (1000, 250)]
LN_GROUPS = [(0, 2), (2, 6), (6, 10)]
ZC = [(0, 512), (512, 512), (1024, N - 1024)]
Z_ACT = [(0, 3), (1, 3), (2, 3)]
Z_DVE = [(c, f) for c in range(3) for f in range(FT - 1)]
SLOW_LINKS = 8
EP, EJ = 125, E // 125


def gnn_kernel(nc, x, src, dst, g1, b1, g2, b2, w_conv, b_conv, w_q, w_k, w_v, w_o, proj, out):
    edges = nc.dram_tensor("edges_overlapped", [NROW, 2 * P], I32, kind="Internal").ap()

    with ExitStack() as ctx:
        def sb(name, shape, dt):
            return ctx.enter_context(nc.sbuf_tensor(name, shape, dt))

        def sem(name):
            return ctx.enter_context(nc.semaphore(name))

        bank = [ctx.enter_context(nc.psum_tensor(f"bank{i}", [P, 512], F32)) for i in range(8)]

        r1 = sb("r1", [P, FT * N], F32)
        r2 = sb("r2", [P, 5120], F32)
        r3 = sb("r3", [P, NT * N // 2], F32)
        r4 = sb("r4", [P, 2 * N], F32)
        wq = r1[:, 0:2048].rearrange("p (t n) -> p t n", t=FT)
        wk = r1[:, 2048:4096].rearrange("p (t n) -> p t n", t=FT)
        aggT = r1[:, :].rearrange("p (t n) -> p t n", t=FT)
        kf = r2[:, 0:4096].rearrange("p (t h m) -> p t h m", t=AT, h=HEADS)
        kT = r2[:, 4096:5120].rearrange("p (t n) -> p t n", t=FT)
        yT = r2[:, 0:FT * N].rearrange("p (t n) -> p t n", t=FT)
        qfT = r3[:, 0:4096].rearrange("p (t h n) -> p t h n", t=2, h=HEADS)
        wv = r3[:, 4096:6144].rearrange("p (t n) -> p t n", t=FT)
        A16 = r3[:, :].bitcast(F16).rearrange("p (a n) -> p a n", a=NT)
        sq = r4[:, 0:2048].rearrange("p (q t n) -> p q t n", q=2, t=FT)
        deg = r4[:, 0:N]
        rdeg = r4[:, N:2 * N]

        xs = sb("xs", [P, NT, D], F32)
        hring = sb("hring", [P, 2, D], F32)
        h1 = sb("h1", [P, NT, D], F16)
        h2 = sb("h2", [P, NT, D], F16)
        hT = sb("hT", [P, FT, N], F32)
        wc = sb("wc", [P, FT, D], F32)
        wo = sb("wo", [P, FT, D], F32)
        ohb = sb("ohb", [P, RING, P], F16)
        ohv = sb("ohv", [P, RING, NT * W], F16)
        qT = sb("qT", [P, FT, NA], F32)
        v1 = sb("v1", [P, AT, HEADS, DH + 1], F32)
        qe = sb("qe", [P, 4, AT, M], F32)
        kv = sb("kv", [P, 2, HEADS, DH + 1], F32)
        attn = qe[:, 0:2, :, :].rearrange("p q t m -> p q (t m)")
        attnT = qe[:, 2:4, :, :].rearrange("p q t m -> p (q t) m")
        haT = sb("haT", [P, FT, NA], F32)
        ind = sb("ind", [P, N], BF16)

        edst = sb("edst", [EP, EJ], I32)
        esrc = sb("esrc", [EP, EJ], I32)
        tail = r2[0:1, 2848:2848 + 2 * TAILN].bitcast(I32).rearrange("p (k n) -> p k n", k=2)
        iota_i = sb("iota_i", [P, NT * W], I32)
        iota16 = sb("iota16", [P, NT * W], F16)
        thr_i = sb("thr_i", [P, NW], I32)
        thr = sb("thr", [P, NW], F32)
        rowc_i = sb("rowc_i", [P, 4], I32)
        rowc = sb("rowc", [P, 4], F32)
        below = r2[0:EP, 2048:2548].rearrange("p (w j) -> p w j", w=NW)
        nbelow = r2[0:EP, 2560:2610]
        nbelow4 = r2[0:EP, 2624:2824].rearrange("p (w k) -> p w k", w=NW)
        edstf = r2[0:EP, 2832:2842]
        first = sb("first", [P, 2], F32)
        rows = sb("rows", [P, 2], I32)
        g = r2[0:HALF, 0:512].bitcast(I32).rearrange("p (q e) -> p q e", q=2)
        gb_i = r2[0:HALF, 512:768].bitcast(I32).rearrange("p (q e) -> p q e", q=2)
        ga_i = r2[0:HALF, 768:1024].bitcast(I32).rearrange("p (q e) -> p q e", q=2)
        gb = r2[0:HALF, 1024:1280].rearrange("p (q e) -> p q e", q=2)
        gd = r2[0:HALF, 1280:1536].rearrange("p (q e) -> p q e", q=2)
        gx = r2[0:HALF, 1536:1792].rearrange("p (q e) -> p q e", q=2)
        gv = r2[0:HALF, 1792:2048].rearrange("p (q e) -> p q e", q=2)
        nout = sb("nout", [HALF, 1], F32)
        bcol = sb("bcol", [P, NSTEP], F32)
        vcol = sb("vcol", [P, NSTEP], F32)
        bnow = sb("bnow", [P, 2, RING], F32)
        vnow = sb("vnow", [P, 2, RING], F32)
        fl = sb("fl", [1, 2], F32)
        flag = sb("flag", [1, 1], I32)

        ident = sb("ident", [P, P], F32)
        ones = sb("ones", [P, P], F32)
        c2048 = sb("c2048", [P, P], F16)
        half2 = sb("half2", [P, 2], F32)
        vrow = sb("vrow", [20, P], F32)
        vec = sb("vec", [P, 20], F32)
        pj = sb("pj", [P, 2, 2 * DH], F32)
        pT = sb("pT", [P, M], F32)
        st = sb("st", [P, NT, 6], F32)
        mv = sb("mv", [P, NT, 2], F32)
        lnw = sb("lnw", [P, 4, NT], F32)
        st1 = sb("st1", [P, FT, 3, 6], F32)
        mv1 = sb("mv1", [P, FT, 2], F32)
        bw = sb("bw", [P, 6, FT], F32)
        s1 = sb("s1", [P, FT], F32)
        t1 = sb("t1", [P, FT], F32)
        s2 = sb("s2", [P, FT], F32)
        t2 = sb("t2", [P, FT], F32)
        twp = sb("twp", [P, FT, 3], F32)
        twb = sb("twb", [P, FT, 3], BF16)
        twr = sb("twr", [P, FT, 1], F32)
        tw3 = sb("tw3", [3, D], BF16)
        mxk = sb("mxk", [P, AT, HEADS], F32)
        mxk1 = sb("mxk1", [P, HEADS], F32)
        mk8 = sb("mk8", [HEADS, 1], F32)
        dg8 = sb("dg8", [HEADS, HEADS], F32)
        mxq = sb("mxq", [P, AT, HEADS], F32)
        diag = sb("diag", [P, 2, AT, HEADS], F32)
        kb = sb("kb", [P, AT, HEADS], F32)
        qb = sb("qb", [P, AT, HEADS], F32)
        zz = sb("zz", [P, 4, 4], F32)
        zr = sb("zr", [P, 4, 4], F32)

        si = r2[0:EP, 0:2 * EJ].bitcast(I32).rearrange("p (k j) -> p k j", k=2)
        sa = r2[0:EP, 2 * EJ:3 * EJ]
        sbb = r2[0:EP, 3 * EJ:4 * EJ]
        sd = r2[0:EP, 4 * EJ:5 * EJ]
        sx = r2[0:EP, 5 * EJ:6 * EJ]
        sv = r2[0:EP, 6 * EJ:7 * EJ]
        sw = r2[0:EP, 7 * EJ:8 * EJ]
        wbase = sb("wbase", [EP, 1], F32)
        aw = sb("aw", [P, 2, NT, W], F16)
        zero16 = sb("zero16", [P, NT * W], F16)

        V_G1, V_B1, V_G2, V_B2, V_BC = range(5)

        order = [("vec", 7), ("proj", 6)]
        order += [(("hT", i), 2 + i % 4) for i in range(NT)]
        order += [("first", 6), ("cols", 7), ("out", 6)]
        order += [(("q", i), 2 + i) for i in range(2)] + [(("k", i), 4 + i) for i in range(2)]
        order += [(("v", i), 6 + i) for i in range(2)]
        order += [("diag", 2)]
        order += [(("uk", i), 3 + i % 4) for i in range(8)]
        order += [("kmaxT", 7), ("tw", 2), ("twT", 2), ("kmax", 7)]
        order += [(("uq", i), 3 + i % 4) for i in range(8)]
        order += [(("qfT", h), 2 if h % 2 else 7) for h in range(HEADS)]
        order += [(("kv", i), 3 + i) for i in range(4)]
        order += [(("attn", i), 3 + i) for i in range(4)]
        order += [(("attnT", i), (2, 7)[i]) for i in range(2)]
        order += [(("ha", i), 3 + i) for i in range(2)]
        order_after = [(("conv", c, f), (7 + c * FT + f) % 8) for c in range(3) for f in range(FT)]
        order_after += [(("zT", i), (3 + i) % 8) for i in range(NT)]
        uses = {}
        nuse = [0] * 8
        for name, b in order + order_after:
            nuse[b] += 1
            uses[name] = (b, nuse[b])
        bank_full = [sem(f"bank_full{b}") for b in range(8)]
        bank_read = [sem(f"bank_read{b}") for b in range(8)]

        def pe_open(pe, name):
            b, n = uses[name]
            if n > 1:
                pe.wait_ge(bank_read[b], n - 1)
            return bank[b]

        def full(name):
            return bank_full[uses[name][0]]

        def read(name):
            return bank_read[uses[name][0]]

        def stored(eng, name):
            b, n = uses[name]
            eng.wait_ge(bank_read[b], n)

        def landed(eng, name):
            b, n = uses[name]
            eng.wait_ge(bank_full[b], n)
            return bank[b]

        x_in = [sem(f"x_in{i}") for i in range(NT)]
        pad_zero = sem("pad_zero")
        e_in = sem("e_in")
        tail_set = sem("tail_set")
        tail_in = sem("tail_in")
        ov_out = sem("ov_out")
        vec_in = sem("vec_in")
        pj_in = sem("pj_in")
        wq_in = sem("wq_in")
        wk_in = sem("wk_in")
        wv_in = sem("wv_in")
        wo_in = sem("wo_in")
        wc_in = sem("wc_in")
        id_set = sem("id_set")
        cst_set = sem("cst_set")
        dve_cst = sem("dve_cst")
        iota_set = sem("iota_set")
        ln_var = sem("ln_var")
        ln_std = sem("ln_std")
        ln_ready = sem("ln_ready")
        h_ready = sem("h_ready")
        h_split = sem("h_split")
        rows_ready = sem("rows_ready")
        g_in = [sem(f"g_in{i}") for i in range(2)]
        g_ready = sem("g_ready")
        nb_ready = sem("nb_ready")
        cols_ready = sem("cols_ready")
        flag_ready = sem("flag_ready")
        vec_ready = sem("vec_ready")
        pT_ready = sem("pT_ready")
        hT_ready = sem("hT_ready")
        qk_ready = sem("qk_ready")
        sq_ready = sem("sq_ready")
        v_ready = sem("v_ready")
        uk_copied = sem("uk_copied")
        kmax_part = sem("kmax_part")
        kmax_diag = sem("kmax_diag")
        k_exp = sem("k_exp")
        kf_ready = sem("kf_ready")
        qb_ready = sem("qb_ready")
        q_exp = sem("q_exp")
        qe_used = sem("qe_used")
        qfT_ready = sem("qfT_ready")
        kv_ready = sem("kv_ready")
        attn_ready = sem("attn_ready")
        attnT_ready = sem("attnT_ready")
        haT_ready = sem("haT_ready")
        hTa_ready = sem("hTa_ready")
        bn_var = sem("bn_var")
        bn_std = sem("bn_std")
        t1_ready = sem("t1_ready")
        twp_ready = sem("twp_ready")
        wc_ready = sem("wc_ready")
        oh_ready = sem("oh_ready")
        win_counted = sem("win_counted")
        pair_stored = sem("pair_stored")
        agg_full = sem("agg_full")
        agg_read = sem("agg_read")
        agg_stored = sem("agg_stored")
        agg_scaled = sem("agg_scaled")
        relu_ready = sem("relu_ready")
        y_ready = sem("y_ready")
        st2_ready = sem("st2_ready")
        z_act = sem("z_act")
        z_dve = sem("z_dve")
        o_ready = sem("o_ready")
        o_out = sem("o_out")
        s_oh = sem("s_oh")
        s_used = sem("s_used")
        s_link = sem("s_link")
        s_prep = sem("s_prep")
        s_count = sem("s_count")
        s_aw = sem("s_aw")
        s_agg = sem("s_agg")
        s_read = sem("s_read")
        dve_step = sem("dve_step")
        act_step = sem("act_step")
        pool_step = sem("pool_step")

        block = ctx.enter_context(nc.Block())

        @block.sync
        def _(sp):
            sp.dma_start(edst[:, :], dst.rearrange("(p j) -> p j", p=EP)).then_inc(e_in, 16)
            for i in range(NT):
                n = P if i < NT - 1 else LAST
                if i == NT - 1:
                    sp.wait_ge(pad_zero, 1)
                sp.dma_start(xs[0:n, i, :], x[i * P:i * P + n, :]).then_inc(x_in[i], 16)
                if i == 3:
                    sp.dma_start(wq, w_q.rearrange("(t p) n -> p t n", p=P)).then_inc(wq_in, 16)
            sp.dma_start(wk, w_k.rearrange("(t p) n -> p t n", p=P)).then_inc(wk_in, 16)
            sp.dma_start(wv, w_v.rearrange("(t p) n -> p t n", p=P)).then_inc(wv_in, 16)
            sp.dma_start(wo[:, :, :], w_o.rearrange("(t p) n -> p t n", p=P)).then_inc(wo_in, 16)
            sp.dma_start(wc[:, :, :], w_conv.rearrange("(t p) n -> p t n", p=P)).then_inc(wc_in, 16)
            for i in range(NT):
                n = P if i < NT - 1 else LAST
                sp.wait_ge(o_ready, i + 1)
                sp.dma_start(out[i * P:i * P + n, :], xs[0:n, i, :]).then_inc(o_out, 16)
            sp.wait_ge(o_out, 16 * NT)

        @block.gpsimd
        def _(pool):
            pool.memset(tail[:, :, :], -1).then_inc(tail_set, 1)
            pool.memset(xs[:, NT - 1, :], 0.0).then_inc(pad_zero, 1)
            pool.iota(thr_i[:, :], [[W, NW]], base=0, channel_multiplier=0).then_inc(iota_set, 1)
            pool.iota(rowc_i[:, 0:1], [[0, 1]], base=0, channel_multiplier=1).then_inc(iota_set, 1)
            pool.iota(iota_i[:, :], [[1, NT * W]], base=0, channel_multiplier=0).then_inc(iota_set, 1)
            pool.memset(ident[:, :], 0.0).then_inc(pool_step, 1)
            pool.wait_ge(pool_step, 1)
            pool.affine_select(out=ident[:, :], in_=ident[:, :], compare_op=ALU.not_equal, fill=1.0, base=0,
                               pattern=[[-1, P]], channel_multiplier=1).then_inc(id_set, 1)
            pool.memset(v1[:, :, :, DH:DH + 1], 1.0).then_inc(cst_set, 1)
            pool.memset(c2048[:, :], HSCALE).then_inc(cst_set, 1)
            pool.memset(zero16[:, :], 0.0).then_inc(cst_set, 1)
            pool.memset(half2[:, :], 0.0).then_inc(pool_step, 1)
            pool.wait_ge(pool_step, 2)
            pool.memset(half2[0:DH, 0:1], 0.5).then_inc(cst_set, 1)
            pool.memset(half2[DH:P, 1:2], 0.5).then_inc(cst_set, 1)
            pool.wait_ge(ov_out, 16 * 4)
            pool.wait_ge(rows_ready, 1)
            for hf in range(2):
                pool.indirect_dma_start(out=g[:, hf, :], out_offset=None, in_=edges,
                                        in_offset=bass.IndirectOffsetOnAxis(ap=rows[0:HALF, hf:hf + 1], axis=0),
                                        ).then_inc(g_in[hf], 16)

        @block.scalar
        def _(act):
            for k, e in enumerate((src, dst)):
                act.dma_start(edges[0:FULL, k * P:(k + 1) * P],
                              bass.AP(e.tensor, 0, [[GR, FULL], [1, P]])).then_inc(ov_out, 16)
            act.wait_ge(tail_set, 1)
            for k, e in enumerate((src, dst)):
                act.dma_start(tail[:, k, 0:E - TAIL0], e[TAIL0:E].rearrange("(o n) -> o n", o=1)).then_inc(tail_in, 16)
            for k, v in enumerate((g1, b1, g2, b2, b_conv)):
                act.dma_start(vrow[4 * k:4 * k + 4, :], v.rearrange("(t p) -> t p", p=P)).then_inc(vec_in, 16)
            for k in range(2):
                act.dma_start(pj[:, :, k * DH:(k + 1) * DH], proj.rearrange("(t p) d -> p t d", p=P)).then_inc(pj_in, 16)
            act.wait_ge(tail_in, 32)
            t_ap = tail[:, :, :]
            for k in range(2):
                act.dma_start(edges[FULL:NROW, k * P:(k + 1) * P].rearrange("(o r) e -> o r e", o=1),
                              bass.AP(t_ap.tensor, t_ap.offset + k * TAILN, [list(t_ap.ap[0]), [GR, NROW - FULL], [1, P]])
                              ).then_inc(ov_out, 16)
            act.dma_start(esrc[:, :], src.rearrange("(p j) -> p j", p=EP)).then_inc(e_in, 16)

            def store_hT(i):
                n = P if i < NT - 1 else LAST
                acc = landed(act, ("hT", i))
                act.activation(hT[:, :, i * P:i * P + n], acc[:, :].rearrange("p (t n) -> p t n", t=FT)[:, :, 0:n],
                               ACT.Copy).then_inc(read(("hT", i)), 1)

            def ln_tiles(gi):
                a, b = LN_GROUPS[gi]
                act.wait_ge(ln_ready, gi + 1)
                for i in range(a, b):
                    if i >= 2:
                        act.wait_ge(h_split, i - 1)
                        act.wait_ge(full(("hT", i - 2)), uses[("hT", i - 2)][1])
                    act.activation(hring[:, i % 2, :], xs[:, i, :], ACT.Relu,
                                   bias=lnw[:, 3, i:i + 1], scale=lnw[:, 2, i:i + 1]).then_inc(h_ready, 1)
                    if i >= 1:
                        store_hT(i - 1)

            for gi, (a, b) in enumerate(LN_GROUPS):
                act.wait_ge(ln_var, gi + 1)
                act.activation(lnw[:, 1, a:b], lnw[:, 0, a:b], ACT.Sqrt).then_inc(ln_std, 1)
                if gi > 0:
                    ln_tiles(gi - 1)
            ln_tiles(len(LN_GROUPS) - 1)
            store_hT(NT - 1)

            for j, (nm, tT) in enumerate((("q", qT), ("k", kT))):
                if j == 1:
                    act.wait_ge(bank_full[uses["cols"][0]], uses["cols"][1])
                for i in range(2):
                    acc = landed(act, (nm, i))
                    act.activation(tT[:, 2 * i:2 * i + 2, :], acc[:, :].rearrange("p (t n) -> p t n", t=2),
                                   ACT.Copy, scale=QK_SCALE).then_inc(read((nm, i)), 1)
                    stored(act, (nm, i))
                    act.activation(sq[:, j, 2 * i:2 * i + 2, :], tT[:, 2 * i:2 * i + 2, :], ACT.Square).then_inc(sq_ready, 1)
            act.wait_ge(bn_var, 1)
            act.activation(bw[:, 1, :], bw[:, 0, :], ACT.Sqrt).then_inc(bn_std, 1)
            for h in range(HEADS):
                acc = landed(act, ("uk", h))
                act.activation(kf[:, :, h, :], acc[:, :].rearrange("p (t m) -> p t m", t=AT),
                               ACT.Copy).then_inc(read(("uk", h)), 1)

            def k_exps(t):
                for h in range(HEADS):
                    act.activation(kf[:, t, h, :], kf[:, t, h, :], ACT.Exp, bias=kb[:, t, h:h + 1]).then_inc(k_exp, 1)

            for h in range(HEADS):
                acc = landed(act, ("uq", h))
                act.wait_ge(qb_ready, h + 1)
                if h >= 4:
                    act.wait_ge(full(("qfT", h - 4)), uses[("qfT", h - 4)][1])
                act.activation(qe[:, h % 4, 0, :], acc[:, 0:M], ACT.Exp, bias=qb[:, 0, h:h + 1])
                act.activation(qe[:, h % 4, 1, :], acc[:, M:2 * M], ACT.Exp, bias=qb[:, 1, h:h + 1]).then_inc(read(("uq", h)), 1)
                if h == 1:
                    stored(act, "kmax")
                    k_exps(0)
                if h == 3:
                    k_exps(1)

            act.wait_ge(flag_ready, 1)
            covered = act.value_load(flag[0:1, 0:1], min_val=0, max_val=1)
            with act.If(covered == 1):
                def store(p, b):
                    act.wait_ge(win_counted, 2 * (p + 1))
                    act.activation(A16[:, :, ds(p * 2 * W, 2 * W)].rearrange("p a (q d) -> p q a d", q=2),
                                   bank[b][:, 0:2 * NT * W].rearrange("p (q a d) -> p q a d", q=2, a=NT),
                                   ACT.Copy).then_inc(pair_stored, 1)

                def store_chunk(c):
                    c0, cn = CHUNKS[c]
                    act.wait_ge(agg_full, c + 1)
                    for f in range(FT):
                        act.activation(aggT[:, f, c0:c0 + cn], bank[2 + f][:, 0:cn], ACT.Copy).then_inc(agg_read, 1)
                    act.activation(deg[:, c0:c0 + cn], bank[6][:, 0:cn], ACT.Copy).then_inc(agg_read, 1)

                with act.Fori(0, 10) as j:
                    for b in range(2):
                        store(2 * j + b, b)
                store_chunk(0)
                for p in range(20, NPAIR):
                    store(p, p % 2)
                store_chunk(1)
                store_chunk(2)

            for c, (c0, cn) in enumerate(CHUNKS):
                for f in range(FT):
                    acc = landed(act, ("conv", c, f))
                    act.activation(yT[:, f, c0:c0 + cn], acc[:, 0:cn], ACT.Relu,
                                   bias=vec[:, 4 * V_BC + f:4 * V_BC + f + 1]).then_inc(read(("conv", c, f)), 1)
            act.wait_ge(bn_var, 2)
            act.activation(bw[:, 1, :], bw[:, 0, :], ACT.Sqrt).then_inc(bn_std, 1)
            act.wait_ge(st2_ready, 1)
            for c, f in Z_ACT:
                c0, cn = ZC[c]
                act.activation(yT[:, f, c0:c0 + cn], yT[:, f, c0:c0 + cn], ACT.Identity,
                               bias=t2[:, f:f + 1], scale=s2[:, f:f + 1]).then_inc(z_act, 1)

        @block.tensor
        def _(pe):
            pe.wait_ge(id_set, 1)
            pe.wait_ge(vec_in, 16 * 5)
            acc = pe_open(pe, "vec")
            nc.tensor.transpose(acc[:, 0:20], vrow[:, :], ident[0:20, 0:20]).then_inc(full("vec"), 1)
            pe.wait_ge(pj_in, 32)
            acc = pe_open(pe, "proj")
            for t in range(2):
                last = nc.tensor.transpose(acc[:, t * P:(t + 1) * P], pj[:, t, :], ident[:, :])
            last.then_inc(full("proj"), 1)

            def transpose_h(i):
                pe.wait_ge(h_ready, i + 1)
                acc = pe_open(pe, ("hT", i))
                for f in range(FT):
                    last = nc.tensor.transpose(acc[:, f * P:(f + 1) * P], hring[:, i % 2, f * P:(f + 1) * P], ident[:, :])
                last.then_inc(full(("hT", i)), 1)

            for i in range(2):
                transpose_h(i)
            pe.wait_ge(nb_ready, 1)
            acc = pe_open(pe, "first")
            for hf in range(2):
                last = nc.tensor.matmul(acc[0:HALF, hf:hf + 1],
                                        nbelow4[:, hf * NW // 2:(hf + 1) * NW // 2, :].rearrange("p w k -> p (w k)"),
                                        ones[0:EP, 0:1], start=True, stop=True)
            last.then_inc(full("first"), 1)
            for i in range(2, NT):
                transpose_h(i)
            pe.wait_ge(g_ready, 1)
            acc = pe_open(pe, "cols")
            for j, m in enumerate((gb, gv)):
                for hf in range(2):
                    o = (2 * j + hf) * HALF
                    last = nc.tensor.transpose(acc[:, o:o + HALF], m[:, hf, :], ident[0:HALF, 0:HALF])
            last.then_inc(full("cols"), 1)
            acc = pe_open(pe, "out")
            nc.tensor.matmul(acc[0:1, 0:1], nout[:, 0:1], ones[0:HALF, 0:1], start=True, stop=True).then_inc(full("out"), 1)

            for i in range(2):
                stored(pe, ("hT", i))
            for nm, w, w_in in (("q", wq, wq_in), ("k", wk, wk_in)):
                pe.wait_ge(w_in, 16)
                for i in range(2):
                    acc = pe_open(pe, (nm, i))
                    for t in range(2):
                        c = (2 * i + t) * P
                        for f in range(FT):
                            last = nc.tensor.matmul(acc[:, t * NA:(t + 1) * NA], w[:, f, c:c + P], hT[:, f, 0:NA],
                                                    start=(f == 0), stop=(f == FT - 1))
                    last.then_inc(full((nm, i)), 1)
            pe.wait_ge(wv_in, 16)
            for t in range(AT):
                acc = pe_open(pe, ("v", t))
                for f in range(FT):
                    last = nc.tensor.matmul(acc[:, :], hT[:, f, t * P:(t + 1) * P], wv[:, f, :],
                                            start=(f == 0), stop=(f == FT - 1))
                last.then_inc(full(("v", t)), 1)
            pe.wait_ge(sq_ready, 4)
            pe.wait_ge(cst_set, 5)
            acc = pe_open(pe, "diag")
            for j in range(2):
                for t in range(AT):
                    for c in range(FT):
                        o = (j * AT + t) * HEADS + 2 * c
                        last = nc.tensor.matmul(acc[:, o:o + 2], sq[:, j, c, t * P:(t + 1) * P], half2[:, :],
                                                start=True, stop=True)
            last.then_inc(full("diag"), 1)

            def features(nm, tT, h):
                p0 = h % 2 * DH
                acc = pe_open(pe, (nm, h))
                for t in range(AT):
                    last = nc.tensor.matmul(acc[:, t * M:(t + 1) * M], tT[p0:p0 + DH, h // 2, t * P:(t + 1) * P],
                                            pT[p0:p0 + DH, :], start=True, stop=True)
                last.then_inc(full((nm, h)), 1)

            def transpose_qf(h):
                acc = pe_open(pe, ("qfT", h))
                stored(pe, ("uq", h))
                for m in range(2):
                    for t in range(2):
                        o = (2 * m + t) * P
                        last = nc.tensor.transpose(acc[:, o:o + P], qe[:, h % 4, t, m * P:(m + 1) * P], ident[:, :])
                last.then_inc(full(("qfT", h)), 1)

            stored(pe, "proj")
            for i in range(8):
                features("uk", kT, i)
            pe.wait_ge(kmax_part, 1)
            acc = pe_open(pe, "kmaxT")
            nc.tensor.transpose(acc[0:HEADS, 0:P], mxk1[:, :], ident[:, :]).then_inc(full("kmaxT"), 1)
            pe.wait_ge(t1_ready, 1)
            pe.wait_ge(wc_in, 16)
            acc = pe_open(pe, "tw")
            for o in range(FT):
                for f in range(FT):
                    last = nc.tensor.matmul(acc[:, o:o + 1], wc[:, f, o * P:(o + 1) * P], t1[:, f:f + 1],
                                            start=(f == 0), stop=(f == FT - 1))
            last.then_inc(full("tw"), 1)
            pe.wait_ge(kmax_diag, 1)
            acc = pe_open(pe, "kmax")
            nc.tensor.matmul(acc[:, 0:HEADS], ones[0:HEADS, :], dg8[:, :], start=True, stop=True).then_inc(full("kmax"), 1)
            for i in range(4):
                features("uq", qT, i)
            pe.wait_ge(twp_ready, 1)
            acc = pe_open(pe, "twT")
            for o in range(FT):
                last = nc.tensor.transpose(acc[0:3, o * P:(o + 1) * P], twp[:, o, :], ident[:, :])
            last.then_inc(full("twT"), 1)
            for hp in range(4):
                transpose_qf(2 * hp)
                transpose_qf(2 * hp + 1)
                if hp < 2:
                    features("uq", qT, 2 * hp + 4)
                    features("uq", qT, 2 * hp + 5)

            for i in range(4):
                m, half = divmod(i, 2)
                acc = pe_open(pe, ("kv", i))
                pe.wait_ge(kf_ready, 2)
                stored(pe, ("v", 0))
                stored(pe, ("v", 1))
                for j in range(4):
                    h = 4 * half + j
                    for t in range(AT):
                        last = nc.tensor.matmul(acc[:, j * (DH + 1):(j + 1) * (DH + 1)], kf[:, t, h, m * P:(m + 1) * P],
                                                v1[:, t, h, :], start=(t == 0), stop=(t == AT - 1))
                last.then_inc(full(("kv", i)), 1)
            for h in range(HEADS):
                stored(pe, ("qfT", h))
            for i in range(4):
                stored(pe, ("kv", i))
            for i in range(4):
                t, half = divmod(i, 2)
                acc = pe_open(pe, ("attn", i))
                for j in range(4):
                    h = 4 * half + j
                    for m in range(2):
                        last = nc.tensor.matmul(acc[:, j * (DH + 1):(j + 1) * (DH + 1)], qfT[:, m, h, t * P:(t + 1) * P],
                                                kv[:, m, h, :], start=(m == 0), stop=(m == 1))
                last.then_inc(full(("attn", i)), 1)
            for i in range(4):
                stored(pe, ("attn", i))
            for i in range(2):
                acc = pe_open(pe, ("attnT", i))
                for c in range(2):
                    for t in range(AT):
                        o = (2 * c + t) * P
                        last = nc.tensor.transpose(acc[:, o:o + P], attn[:, t, (2 * i + c) * P:(2 * i + c + 1) * P], ident[:, :])
                last.then_inc(full(("attnT", i)), 1)
            pe.wait_ge(wo_in, 16)
            for i in range(2):
                stored(pe, ("attnT", i))
            for i in range(2):
                acc = pe_open(pe, ("ha", i))
                for t in range(2):
                    o = (2 * i + t) * P
                    for c in range(FT):
                        last = nc.tensor.matmul(acc[:, t * NA:(t + 1) * NA], wo[:, c, o:o + P], attnT[:, c, :],
                                                start=(c == 0), stop=(c == FT - 1))
                last.then_inc(full(("ha", i)), 1)

            for i in range(2):
                stored(pe, ("ha", i))
            pe.wait_ge(h_split, NT)
            pe.wait_ge(flag_ready, 1)
            covered = pe.value_load(flag[0:1, 0:1], min_val=0, max_val=1)
            with pe.If(covered == 1):
                def count(p, b, wait):
                    if wait:
                        pe.wait_ge(pair_stored, p - 1)
                    for q in range(2):
                        pe.wait_ge(oh_ready, 2 * p + q + 1)
                        for k in range(K):
                            s = (2 * b + q) * K + k
                            last = nc.tensor.matmul(bank[b][:, q * NT * W:(q + 1) * NT * W], ohb[:, s, :], ohv[:, s, :],
                                                    start=(k == 0), stop=(k == K - 1))
                        if q == 0:
                            last.then_inc(win_counted, 1)
                    last.then_inc(win_counted, 1)

                def aggregate(c, s, first, last_):
                    c0, cn = CHUNKS[c]
                    for f in range(FT):
                        for hh in (h1, h2):
                            nc.tensor.matmul(bank[2 + f][:, 0:cn], hh[:, s, f * P:(f + 1) * P], A16[:, s, c0:c0 + cn],
                                             start=(first and hh is h1), stop=(last_ and hh is h2))
                    last = nc.tensor.matmul(bank[6][:, 0:cn], c2048[:, :], A16[:, s, c0:c0 + cn], start=first, stop=last_)
                    if last_:
                        last.then_inc(agg_full, 1)

                count(0, 0, False)
                count(1, 1, False)
                with pe.Fori(1, 5) as j:
                    for b in range(2):
                        count(2 * j + b, b, True)
                count(10, 0, True)
                count(11, 1, True)
                pe.wait_ge(pair_stored, 10)
                aggregate(0, 0, True, False)
                aggregate(0, 1, False, False)
                with pe.Fori(6, 9) as j:
                    for b in range(2):
                        count(2 * j + b, b, True)
                        for f in range(FT):
                            for hh in (h1, h2):
                                nc.tensor.matmul(bank[2 + f][:, 0:500],
                                                 hh[:, ds(2 * j + (b - 10), 1), f * P:(f + 1) * P].rearrange("p o n -> p (o n)"),
                                                 A16[:, ds(2 * j + (b - 10), 1), 0:500].rearrange("p o n -> p (o n)"),
                                                 start=False, stop=False)
                        nc.tensor.matmul(bank[6][:, 0:500], c2048[:, :],
                                         A16[:, ds(2 * j + (b - 10), 1), 0:500].rearrange("p o n -> p (o n)"),
                                         start=False, stop=False)
                count(18, 0, True)
                aggregate(0, 8, False, False)
                count(19, 1, True)
                aggregate(0, 9, False, True)
                pe.wait_ge(pair_stored, 18)
                count(20, 0, True)
                count(21, 1, True)
                pe.wait_ge(pair_stored, 20)
                pe.wait_ge(agg_read, FT + 1)
                for s in range(4):
                    aggregate(1, s, s == 0, False)
                count(22, 0, True)
                count(23, 1, True)
                for s in range(4, 7):
                    aggregate(1, s, False, False)
                count(24, 0, True)
                for s in range(7, NT):
                    aggregate(1, s, False, s == NT - 1)
                pe.wait_ge(pair_stored, NPAIR)
                pe.wait_ge(agg_read, 2 * (FT + 1))
                for s in range(NT):
                    aggregate(2, s, s == 0, s == NT - 1)
            with pe.Else():
                with pe.Fori(0, NW) as w:
                    nc.tensor.matmul(bank[0][:, 0:NT * W], zero16[:, 0:P], zero16[:, :], start=True, stop=False)
                    with pe.Fori(0, EJ // 8) as gg:
                        pe.wait_ge(s_oh, w * (EJ // 8) + gg + 1)
                        for s in range(8):
                            last = nc.tensor.matmul(bank[0][:, 0:NT * W], ohb[0:EP, s, :], ohv[0:EP, s, :],
                                                    start=False, stop=False)
                        last.then_inc(s_used, 1)
                    nc.tensor.matmul(bank[0][:, 0:NT * W], zero16[:, 0:P], zero16[:, :], start=False, stop=True).then_inc(s_count, 1)
                    pe.wait_ge(s_aw, w + 1)
                    for f in range(FT + 1):
                        for s in range(NT):
                            for hl in range(2):
                                for hh in (h1, h2) if f < FT else (c2048,):
                                    lhs = hh[:, s, f * P:(f + 1) * P] if f < FT else c2048[:, :]
                                    last = nc.tensor.matmul(bank[2 + f][:, 0:W], lhs, aw[:, hl, s, :],
                                                            start=(s == 0 and hl == 0 and hh is not h2),
                                                            stop=(s == NT - 1 and hl == 1 and hh is not h1))
                    last.then_inc(s_agg, 1)
                    pe.wait_ge(s_read, w + 1)

            pe.wait_ge(wc_ready, 1)
            stored(pe, "twT")
            n_conv = 0
            for c, (c0, cn) in enumerate(CHUNKS):
                pe.wait_ge(agg_scaled, c + 1)
                for o in range(FT):
                    acc = pe_open(pe, ("conv", c, o))
                    if n_conv == 3:
                        pe.wait_ge(agg_read, 3 * (FT + 1))
                    n_conv += 1
                    for f in range(FT):
                        nc.tensor.matmul(acc[:, 0:cn], wc[:, f, o * P:(o + 1) * P], aggT[:, f, c0:c0 + cn],
                                         start=(f == 0), stop=False)
                    nc.tensor.matmul(acc[:, 0:cn], tw3[:, o * P:(o + 1) * P], ind[0:3, c0:c0 + cn],
                                     start=False, stop=True).then_inc(full(("conv", c, o)), 1)
            for i in range(NT):
                n = P if i < NT - 1 else LAST
                c = i * P // 512
                pe.wait_ge(z_dve, sum(1 for cc, _ in Z_DVE if cc <= c))
                pe.wait_ge(z_act, sum(1 for cc, _ in Z_ACT if cc <= c))
                if i < 8:
                    acc = pe_open(pe, ("zT", i))
                else:
                    pe.wait_ge(o_ready, i - 7)
                    acc = bank[uses[("zT", i)][0]]
                for f in range(FT):
                    last = nc.tensor.transpose(acc[0:n, f * P:(f + 1) * P], yT[:, f, i * P:i * P + n], ident[:, :])
                last.then_inc(full(("zT", i)), 1)

        @block.vector
        def _(dve):
            V = nc.vector
            step = [0]

            def link(ins):
                step[0] += 1
                ins.then_inc(dve_step, 1)
                dve.wait_ge(dve_step, step[0])

            def rstd(var, std, r, t):
                link(V.reciprocal(r, std))
                link(V.tensor_tensor(t, r, r, ALU.mult))
                link(V.tensor_tensor(t, t, var, ALU.mult))
                link(V.tensor_scalar(t, t, -0.5, 1.5, ALU.mult, ALU.add))
                link(V.tensor_tensor(r, r, t, ALU.mult))

            V.memset(ones[:, :], 1.0).then_inc(dve_cst, 1)
            dve.wait_ge(iota_set, 3)
            link(V.tensor_copy(thr[:, :], thr_i[:, :]))
            link(V.tensor_copy(iota16[:, :], iota_i[:, :]))
            link(V.tensor_scalar(rowc_i[:, 1:2], rowc_i[:, 0:1], K - 1, None, ALU.bitwise_and))
            link(V.tensor_scalar(rowc_i[:, 2:3], rowc_i[:, 0:1], 2, None, ALU.arith_shift_right))
            link(V.tensor_scalar(rowc[:, 0:1], rowc_i[:, 1:2], float(P // GR), None, ALU.mult))
            link(V.tensor_scalar(rowc[:, 1:2], rowc_i[:, 2:3], float(W), None, ALU.mult))
            link(V.tensor_scalar(rowc[:, 2:3], rowc[:, 1:2], float(W * NW // 2), None, ALU.add))
            dve.wait_ge(e_in, 32)
            link(V.tensor_copy(edstf[:, :], edst[:, ::GR]))
            nj = EJ // GR
            link(V.tensor_tensor(below[:, :, :], edstf[:, :].unsqueeze(1).to_broadcast([EP, NW, nj]),
                                 thr[0:EP, :].unsqueeze(2).to_broadcast([EP, NW, nj]), ALU.is_lt))
            link(V.tensor_reduce(nbelow[:, :], below[:, :, :], AX_X, ALU.add))
            V.tensor_copy(nbelow4[:, :, :], nbelow[:, :].unsqueeze(2).to_broadcast([EP, NW, K])).then_inc(nb_ready, 1)

            dve.wait_ge(full("vec"), 1)
            V.tensor_copy(vec[:, :], bank[uses["vec"][0]][:, 0:20]).then_inc(read("vec"), 1)
            dve.wait_ge(full("proj"), 1)
            V.tensor_copy(pT[:, :], bank[uses["proj"][0]][:, 0:M]).then_inc(read("proj"), 1)

            def ln_stats(gi):
                a, b = LN_GROUPS[gi]
                for i in range(a, b):
                    if i == NT - 1:
                        dve.wait_ge(pad_zero, 1)
                    dve.wait_ge(x_in[i], 16)
                    link(V.bn_stats(st[:, i, :], xs[:, i, :]))
                    link(V.bn_aggr(mv[:, i, :], st[:, i, :]))
                V.tensor_scalar(lnw[:, 0, a:b], mv[:, a:b, 1], EPS, None, ALU.add).then_inc(ln_var, 1)

            def ln_scale(gi):
                a, b = LN_GROUPS[gi]
                dve.wait_ge(ln_std, gi + 1)
                rstd(lnw[:, 0, a:b], lnw[:, 1, a:b], lnw[:, 2, a:b], lnw[:, 3, a:b])
                V.scalar_tensor_tensor(out=lnw[:, 3, a:b], in0=mv[:, a:b, 0], scalar=-1.0, in1=lnw[:, 2, a:b],
                                       op0=ALU.mult, op1=ALU.mult).then_inc(ln_ready, 1)

            def split(i):
                dve.wait_ge(h_ready, i + 1)
                link(V.tensor_scalar(h1[:, i, :], hring[:, i % 2, :], HSCALE, None, ALU.mult))
                V.scalar_tensor_tensor(out=h2[:, i, :], in0=hring[:, i % 2, :], scalar=HSCALE, in1=h1[:, i, :],
                                       op0=ALU.mult, op1=ALU.subtract).then_inc(h_split, 1)

            ln_stats(0)
            ln_stats(1)
            ln_scale(0)
            split(0)
            split(1)
            dve.wait_ge(full("first"), uses["first"][1])
            V.tensor_scalar(first[0:HALF, :], bank[uses["first"][0]][0:HALF, 0:2], -1.0, 0.0, ALU.add, ALU.max
                            ).then_inc(read("first"), 1)
            stored(dve, "first")
            V.tensor_scalar(rows[0:HALF, :], first[0:HALF, :], rowc[0:HALF, 0:1], None, ALU.add).then_inc(rows_ready, 1)
            ln_stats(2)
            ln_scale(1)
            for i in range(2, 6):
                split(i)
            ln_scale(2)
            for i in range(6, NT):
                split(i)

            for hf in range(2):
                dve.wait_ge(g_in[hf], 16)
            link(V.tensor_scalar(gb_i[:, :, :], g[:, :, 0:P], P - 1, None, ALU.bitwise_and))
            link(V.tensor_scalar(ga_i[:, :, :], g[:, :, 0:P], 7, None, ALU.arith_shift_right))
            for hf in range(2):
                link(V.tensor_scalar(gd[:, hf, :], g[:, hf, P:2 * P], rowc[0:HALF, 1 + hf:2 + hf], None, ALU.subtract))
            link(V.tensor_copy(gb[:, :, :], gb_i[:, :, :]))
            link(V.tensor_scalar(gx[:, :, :], gd[:, :, :], 0.0, None, ALU.is_lt))
            link(V.scalar_tensor_tensor(out=gx[:, :, :], in0=gd[:, :, :], scalar=W - 0.5, in1=gx[:, :, :],
                                        op0=ALU.is_gt, op1=ALU.add))
            link(V.scalar_tensor_tensor(out=gv[:, :, :], in0=ga_i[:, :, :], scalar=float(W), in1=gd[:, :, :],
                                        op0=ALU.mult, op1=ALU.add))
            link(V.tensor_scalar(gx[:, :, :], gx[:, :, :], 0.5, None, ALU.is_gt, ALU.add, accum_out=nout[:, :]))
            V.scalar_tensor_tensor(out=gv[:, :, :], in0=gx[:, :, :], scalar=4096.0, in1=gv[:, :, :],
                                   op0=ALU.mult, op1=ALU.add).then_inc(g_ready, 1)

            for i in range(NT):
                stored(dve, ("hT", i))
            for f in range(FT):
                for c in range(3):
                    a, b = c * 512, min((c + 1) * 512, N)
                    ins = V.bn_stats(st1[:, f, c, :], hT[:, f, a:b])
            link(ins)
            for f in range(FT):
                ins = V.bn_aggr(mv1[:, f, :], st1[:, f, :, :].rearrange("p c s -> p (c s)"))
            link(ins)
            link(V.tensor_scalar(bw[:, 0, :], mv1[:, :, 1], EPS, None, ALU.add))
            V.tensor_scalar(bw[:, 4, :], mv1[:, :, 1], EPS, None, ALU.add).then_inc(bn_var, 1)

            dve.wait_ge(full("cols"), uses["cols"][1])
            acc = bank[uses["cols"][0]]
            V.tensor_copy(bcol[:, :], acc[:, 0:NSTEP])
            V.tensor_copy(vcol[:, :], acc[:, NSTEP:2 * NSTEP]).then_inc(read("cols"), 1)
            dve.wait_ge(full("out"), uses["out"][1])
            V.tensor_scalar(fl[0:1, 1:2], bank[uses["out"][0]][0:1, 0:1], float(NSTEP * P - E), None, ALU.is_equal
                            ).then_inc(read("out"), 1)
            stored(dve, "out")
            V.tensor_copy(flag[:, :], fl[0:1, 1:2]).then_inc(flag_ready, 1)
            for t in range(AT):
                acc = landed(dve, ("v", t))
                dve.wait_ge(cst_set, 5)
                V.tensor_copy(v1[:, t, :, 0:DH], acc[:, :].rearrange("p (h d) -> p h d", h=HEADS)).then_inc(read(("v", t)), 1)

            dve.wait_ge(bn_std, 1)
            rstd(bw[:, 0, :], bw[:, 1, :], bw[:, 2, :], bw[:, 3, :])
            link(V.tensor_tensor(s1[:, :], vec[:, 4 * V_G1:4 * V_G1 + 4], bw[:, 2, :], ALU.mult))
            link(V.tensor_tensor(bw[:, 3, :], mv1[:, :, 0], s1[:, :], ALU.mult))
            V.tensor_tensor(t1[:, :], vec[:, 4 * V_B1:4 * V_B1 + 4], bw[:, 3, :], ALU.subtract).then_inc(t1_ready, 1)

            acc = landed(dve, "diag")
            V.tensor_copy(diag[:, :, :, :].rearrange("p j t h -> p (j t h)"), acc[:, 0:32]).then_inc(read("diag"), 1)
            stored(dve, "diag")
            for h in range(HEADS):
                stored(dve, ("uk", h))
                ins = V.tensor_reduce(mxk[:, :, h], kf[:, :, h, :], AX_X, ALU.max)
            link(ins)
            V.tensor_tensor(mxk1[:, :], mxk[:, 0, :], mxk[:, 1, :], ALU.max).then_inc(kmax_part, 1)
            acc = landed(dve, "kmaxT")
            V.tensor_reduce(mk8[:, :], acc[0:HEADS, 0:P], AX_X, ALU.max).then_inc(read("kmaxT"), 1)
            stored(dve, "kmaxT")
            V.tensor_scalar(dg8[:, :], ident[0:HEADS, 0:HEADS], mk8[:, 0:1], None, ALU.mult).then_inc(kmax_diag, 1)

            acc = landed(dve, "tw")
            V.tensor_copy(twr[:, :, 0], acc[:, 0:FT]).then_inc(read("tw"), 1)
            stored(dve, "tw")
            for k in range(3):
                link(V.tensor_copy(twb[:, :, k], twr[:, :, 0]))
                ins = V.tensor_copy(twp[:, :, k], twb[:, :, k])
                if k < 2:
                    link(ins)
                    link(V.tensor_tensor(twr[:, :, 0], twr[:, :, 0], twp[:, :, k], ALU.subtract))
            ins.then_inc(twp_ready, 1)

            acc = landed(dve, "kmax")
            for t in range(AT):
                ins = V.scalar_tensor_tensor(out=kb[:, t, :], in0=acc[:, 0:HEADS], scalar=-1.0, in1=diag[:, 1, t, :],
                                             op0=ALU.mult, op1=ALU.subtract)
            ins.then_inc(read("kmax"), 1)

            def q_bias(h):
                acc = landed(dve, ("uq", h))
                link(V.tensor_reduce(mxq[:, :, h], acc[:, :].rearrange("p (t m) -> p t m", t=AT), AX_X, ALU.max))
                V.scalar_tensor_tensor(out=qb[:, :, h], in0=mxq[:, :, h], scalar=-1.0,
                                       in1=diag[:, 0, :, h], op0=ALU.mult, op1=ALU.subtract).then_inc(qb_ready, 1)

            def q_feat(h):
                acc = landed(dve, ("qfT", h))
                if h == 0:
                    for t in range(AT):
                        dve.wait_ge(full(("v", t)), uses[("v", t)][1])
                V.tensor_scalar(qfT[:, :, h, :], acc[:, :].rearrange("p (m n) -> p m n", m=2), PHI_SCALE, KEPS,
                                ALU.mult, ALU.add).then_inc(read(("qfT", h)), 1)

            for i in range(4):
                q_bias(i)
            acc = landed(dve, "twT")
            V.tensor_copy(tw3[:, :], acc[0:3, :]).then_inc(read("twT"), 1)
            for hp in range(4):
                q_feat(2 * hp)
                q_feat(2 * hp + 1)
                if hp < 2:
                    q_bias(2 * hp + 4)
                    q_bias(2 * hp + 5)
                else:
                    t = hp - 2
                    dve.wait_ge(k_exp, HEADS * (t + 1))
                    V.tensor_scalar(kf[:, t, :, :], kf[:, t, :, :], PHI_SCALE, KEPS, ALU.mult, ALU.add).then_inc(kf_ready, 1)
            for i in range(4):
                m, half = divmod(i, 2)
                acc = landed(dve, ("kv", i))
                V.tensor_copy(kv[:, m, 4 * half:4 * half + 4, :], acc[:, 0:4 * (DH + 1)].rearrange("p (h d) -> p h d", h=4)
                              ).then_inc(read(("kv", i)), 1)
            for i in range(4):
                t, half = divmod(i, 2)
                acc = landed(dve, ("attn", i))
                a = acc[:, 0:4 * (DH + 1)].rearrange("p (h d) -> p h d", h=4)
                link(V.tensor_scalar(zz[:, i, :], a[:, :, DH], KEPS, None, ALU.add))
                link(V.reciprocal(zr[:, i, :], zz[:, i, :]))
                V.tensor_tensor(attn[:, t, half * 256:(half + 1) * 256].rearrange("p (h d) -> p h d", h=4), a[:, :, 0:DH],
                                zr[:, i, :].unsqueeze(2).to_broadcast([P, 4, DH]), ALU.mult).then_inc(read(("attn", i)), 1)
            for i in range(2):
                acc = landed(dve, ("attnT", i))
                V.tensor_copy(attnT[:, 2 * i:2 * i + 2, :], acc[:, :].rearrange("p (t n) -> p t n", t=2)
                              ).then_inc(read(("attnT", i)), 1)
            for f in range(FT):
                ins = V.tensor_scalar(wc[:, f, :], wc[:, f, :], s1[:, f:f + 1], None, ALU.mult)
            ins.then_inc(wc_ready, 1)
            for i in range(2):
                acc = landed(dve, ("ha", i))
                V.tensor_copy(haT[:, 2 * i:2 * i + 2, :], acc[:, :].rearrange("p (t n) -> p t n", t=2)
                              ).then_inc(read(("ha", i)), 1)
                stored(dve, ("ha", i))
            V.tensor_tensor(hT[:, :, 0:NA], hT[:, :, 0:NA], haT[:, :, :], ALU.add).then_inc(hTa_ready, 1)

            stored(dve, "cols")
            covered = dve.value_load(flag[0:1, 0:1], min_val=0, max_val=1)
            with dve.If(covered == 1):
                def one_hots(wi, slot, par, wait):
                    if wait:
                        dve.wait_ge(win_counted, wi - RING // K + 1)
                    for k in range(K):
                        s = slot * K + k
                        V.tensor_scalar(ohb[:, s, :], iota16[:, 0:P], bnow[:, par, s:s + 1], None, ALU.is_equal)
                        last = V.tensor_scalar(ohv[:, s, :], iota16[:, :], vnow[:, par, s:s + 1], None, ALU.is_equal)
                    last.then_inc(oh_ready, 1)

                def columns(j, par, n):
                    V.tensor_copy(bnow[:, par, 0:n], bcol[:, ds(j, n)])
                    V.tensor_copy(vnow[:, par, 0:n], vcol[:, ds(j, n)]).then_inc(cols_ready, 1)

                columns(0, 0, RING)
                dve.wait_ge(cols_ready, 1)
                for q in range(4):
                    one_hots(q, q, 0, False)
                with dve.Fori(1, NW // 4) as j:
                    dve.wait_ge(oh_ready, 4 * j)
                    columns(RING * j, 0, RING)
                    dve.wait_ge(cols_ready, j + 1)
                    for q in range(4):
                        one_hots(4 * j + q, q, 0, True)
                n0 = NW // 4 * 4
                dve.wait_ge(oh_ready, n0)
                columns(n0 * K, 0, (NW - n0) * K)
                dve.wait_ge(cols_ready, NW // 4 + 1)
                for q in range(NW - n0):
                    one_hots(n0 + q, q, 0, True)
            with dve.Else():
                nprep = [0]

                def prep(ins):
                    nprep[0] += 1
                    ins.then_inc(s_prep, 1)
                    dve.wait_ge(s_prep, nprep[0])

                prep(V.tensor_scalar(si[:, 0, :], esrc[:, :], 7, None, ALU.arith_shift_right))
                prep(V.tensor_scalar(si[:, 1, :], esrc[:, :], P - 1, None, ALU.bitwise_and))
                prep(V.tensor_copy(sa[:, :], si[:, 0, :]))
                prep(V.tensor_copy(sbb[:, :], si[:, 1, :]))
                prep(V.tensor_copy(sd[:, :], edst[:, :]))
                prep(V.memset(wbase[:, :], 0.0))
                V.memset(fl[0:1, 0:1], 0.0).then_inc(s_used, 1)
                with dve.Fori(0, NW) as w:
                    seq = [0]

                    def chain(ins):
                        seq[0] += 1
                        ins.then_inc(s_link, 1)
                        dve.wait_ge(s_link, w * SLOW_LINKS + seq[0])

                    chain(V.tensor_scalar(sx[:, :], sd[:, :], wbase[:, 0:1], None, ALU.subtract))
                    chain(V.scalar_tensor_tensor(out=sv[:, :], in0=sa[:, :], scalar=float(W), in1=sx[:, :],
                                                 op0=ALU.mult, op1=ALU.add))
                    chain(V.tensor_scalar(sw[:, :], sx[:, :], 0.0, None, ALU.is_lt))
                    chain(V.scalar_tensor_tensor(out=sx[:, :], in0=sx[:, :], scalar=W - 0.5, in1=sw[:, :],
                                                 op0=ALU.is_gt, op1=ALU.add))
                    chain(V.tensor_scalar(sx[:, :], sx[:, :], 4096.0, None, ALU.mult))
                    chain(V.tensor_tensor(sv[:, :], sv[:, :], sx[:, :], ALU.add))
                    seq[0] += 1
                    V.tensor_scalar(wbase[:, :], wbase[:, :], float(W), None, ALU.add).then_inc(s_link, 1)
                    with dve.Fori(0, EJ // 8) as gg:
                        dve.wait_ge(s_used, w * (EJ // 8) + gg + 1)
                        for s in range(8):
                            V.tensor_scalar(ohb[0:EP, s, :], iota16[0:EP, 0:P], sbb[:, ds(8 * gg + s, 1)], None, ALU.is_equal)
                            last = V.tensor_scalar(ohv[0:EP, s, :], iota16[0:EP, :], sv[:, ds(8 * gg + s, 1)], None, ALU.is_equal)
                        last.then_inc(s_oh, 1)
                    dve.wait_ge(s_count, w + 1)
                    cnt = bank[0][:, 0:NT * W].rearrange("p (a d) -> p a d", a=NT)
                    chain(V.tensor_copy(aw[:, 0, :, :], cnt))
                    V.tensor_tensor(aw[:, 1, :, :], cnt, aw[:, 0, :, :], ALU.subtract).then_inc(s_aw, 1)
                    dve.wait_ge(s_agg, w + 1)
                    for f in range(FT):
                        V.tensor_copy(aggT[:, f, ds(W * w, W)], bank[2 + f][:, 0:W])
                    V.tensor_copy(deg[:, ds(W * w, W)], bank[6][:, 0:W]).then_inc(s_read, 1)
                dve.wait_ge(s_read, NW)
                V.memset(fl[0:1, 0:1], 0.0).then_inc(agg_read, 3 * (FT + 1))

            def mean(c):
                c0, cn = CHUNKS[c]
                dve.wait_ge(agg_read, (FT + 1) * (c + 1))
                link(V.tensor_scalar(rdeg[:, c0:c0 + cn], deg[:, c0:c0 + cn], HSCALE, None, ALU.max))
                link(V.reciprocal(rdeg[:, c0:c0 + cn], rdeg[:, c0:c0 + cn]))
                V.tensor_scalar(ind[:, c0:c0 + cn], deg[:, c0:c0 + cn], 1.0, None, ALU.min)
                for f in range(FT):
                    ins = V.tensor_tensor(aggT[:, f, c0:c0 + cn], aggT[:, f, c0:c0 + cn], rdeg[:, c0:c0 + cn], ALU.mult)
                ins.then_inc(agg_scaled, 1)

            ny = [0]

            def add_y(c):
                c0, cn = CHUNKS[c]
                for f in range(FT):
                    stored(dve, ("conv", c, f))
                    own = max(0, min(NA - c0, cn))
                    if own:
                        ins = V.tensor_tensor(yT[:, f, c0:c0 + own], yT[:, f, c0:c0 + own], hT[:, f, c0:c0 + own], ALU.add)
                    ins = V.scalar_tensor_tensor(out=yT[:, f, c0 + own:c0 + cn], in0=hT[:, f, c0 + own:c0 + cn],
                                                 scalar=haT[:, f, NA - 1:NA], in1=yT[:, f, c0 + own:c0 + cn],
                                                 op0=ALU.add, op1=ALU.add)
                    ny[0] += 1
                    ins.then_inc(y_ready, 1)
                    dve.wait_ge(y_ready, ny[0])
                    ins = V.bn_stats(st1[:, f, c, :], yT[:, f, c0:c0 + cn])
                return ins

            dve.wait_ge(hTa_ready, 1)
            mean(0)
            mean(1)
            add_y(0)
            mean(2)
            add_y(1)
            link(add_y(2))
            for f in range(FT):
                ins = V.bn_aggr(mv1[:, f, :], st1[:, f, :, :].rearrange("p c s -> p (c s)"))
            link(ins)
            V.tensor_scalar(bw[:, 0, :], mv1[:, :, 1], EPS, None, ALU.add).then_inc(bn_var, 1)
            dve.wait_ge(bn_std, 2)
            rstd(bw[:, 0, :], bw[:, 1, :], bw[:, 2, :], bw[:, 3, :])
            link(V.tensor_tensor(s2[:, :], vec[:, 4 * V_G2:4 * V_G2 + 4], bw[:, 2, :], ALU.mult))
            link(V.tensor_tensor(bw[:, 3, :], mv1[:, :, 0], s2[:, :], ALU.mult))
            V.tensor_tensor(t2[:, :], vec[:, 4 * V_B2:4 * V_B2 + 4], bw[:, 3, :], ALU.subtract).then_inc(st2_ready, 1)
            dve.wait_ge(st2_ready, 1)

            def z(c):
                for cc, f in Z_DVE:
                    if cc == c:
                        c0, cn = ZC[c]
                        V.tensor_scalar(yT[:, f, c0:c0 + cn], yT[:, f, c0:c0 + cn], s2[:, f:f + 1], t2[:, f:f + 1],
                                        ALU.mult, ALU.add).then_inc(z_dve, 1)

            def finish(i):
                n = P if i < NT - 1 else LAST
                acc = landed(dve, ("zT", i))
                V.tensor_tensor(xs[0:n, i, :], acc[0:n, :], xs[0:n, i, :], ALU.add).then_inc(o_ready, 1)

            z(0)
            z(1)
            for i in range(4):
                finish(i)
            z(2)
            for i in range(4, NT):
                finish(i)


_INS = ['x', 'src', 'dst', 'L0_gnn_norm1_g', 'L0_gnn_norm1_b', 'L0_gnn_norm2_g', 'L0_gnn_norm2_b', 'L0_gnn_W_conv',
        'L0_gnn_b_conv', 'L0_gnn_Wq', 'L0_gnn_Wk', 'L0_gnn_Wv', 'L0_gnn_Wo', 'L0_gnn_proj']


def kernel(**inputs):
    import numpy as _np
    import concourse.bacc as _bacc
    from concourse import mybir as _mybir
    from concourse.bass_utils import run_bass_kernel_spmd as _run

    nc = _bacc.Bacc("TRN2", target_bir_lowering=False, num_devices=1)
    arrays, args = {}, []
    for name in _INS:
        a = _np.ascontiguousarray(inputs[name])
        arrays[f"in_{name}"] = a
        args.append(nc.dram_tensor(f"in_{name}", a.shape, _mybir.dt.from_np(a.dtype), kind="ExternalInput").ap())
    out = nc.dram_tensor("out", (N, D), F32, kind="ExternalOutput").ap()
    gnn_kernel(nc, *args, out)
    r = _run(nc, [arrays], core_ids=[0])
    return r.results[0]["out"]
```

```python
from contextlib import ExitStack

import concourse.bass as bass
from concourse import mybir

ALU = mybir.AluOpType
ACT = mybir.ActivationFunctionType
AX_X = mybir.AxisListType.X
F32 = mybir.dt.float32
F16 = mybir.dt.float16
I32 = mybir.dt.int32
U32 = mybir.dt.uint32
ds = bass.ds

P = 128
N = 1250
D = 512
E = 20000
NT = (N + P - 1) // P
LAST = N - (NT - 1) * P
FT = D // P
HEADS, DH, M = 8, 64, 256
NA = 256
AT = NA // P
EPS, KEPS = 1e-5, 1e-6
QK_SCALE = DH ** -0.25
PHI_SCALE = 1.0 / M ** 0.5

W = 25
NW = N // W
NPAIR = NW // 2
K = 4
CAP = K * P
GR = 16
NSTEP = NW * K
HALF = NSTEP // 2
NROW = E // GR + (K - 1) * P // GR
FULL = (E - P) // GR + 1
TAIL0 = FULL * GR
TAILN = (NROW - FULL - 1) * GR + P
RING = 16
HSCALE = 2048.0
CHUNKS = [(0, 500), (500, 500), (1000, 250)]
LN_GROUPS = [(0, 2), (2, 6), (6, 10)]
ZC = [(0, 512), (512, 512), (1024, N - 1024)]
Z_ACT = [(0, 3), (1, 3), (2, 3)]
Z_DVE = [(c, f) for c in range(3) for f in range(FT - 1)]
SLOW_LINKS = 8
DEG_FIRST = [FT, 0, 1, 2, 3]
EP, EJ = 125, E // 125


def gnn_kernel(nc, x, src, dst, g1, b1, g2, b2, w_conv, b_conv, w_q, w_k, w_v, w_o, proj, out):
    edges = nc.dram_tensor("edges_overlapped", [NROW, 2 * P], I32, kind="Internal").ap()

    with ExitStack() as ctx:
        def sb(name, shape, dt):
            return ctx.enter_context(nc.sbuf_tensor(name, shape, dt))

        def sem(name):
            return ctx.enter_context(nc.semaphore(name))

        bank = [ctx.enter_context(nc.psum_tensor(f"bank{i}", [P, 512], F32)) for i in range(8)]

        r1 = sb("r1", [P, FT * N], F32)
        r2 = sb("r2", [P, 5120], F32)
        r3 = sb("r3", [P, NT * N // 2], F32)
        r4 = sb("r4", [P, 2 * N], F32)
        wq = r1[:, 0:2048].rearrange("p (t n) -> p t n", t=FT)
        wk = r1[:, 2048:4096].rearrange("p (t n) -> p t n", t=FT)
        aggT = r1[:, :].rearrange("p (t n) -> p t n", t=FT)
        kf = r2[:, 0:4096].rearrange("p (t h m) -> p t h m", t=AT, h=HEADS)
        kT = r2[:, 4096:5120].rearrange("p (t n) -> p t n", t=FT)
        yT = r2[:, 0:FT * N].rearrange("p (t n) -> p t n", t=FT)
        qfT = r1[:, 0:4096].rearrange("p (t h n) -> p t h n", t=2, h=HEADS)
        A16 = r3[:, :].bitcast(F16).rearrange("p (a n) -> p a n", a=NT)
        sq = r4[:, 0:2048].rearrange("p (q t n) -> p q t n", q=2, t=FT)
        deg = r4[:, 0:N]
        rdeg = r4[:, N:2 * N]

        xs = sb("xs", [P, NT, D], F32)
        hring = sb("hring", [P, 2, D], F32)
        h1 = sb("h1", [P, NT, D], F16)
        h2 = sb("h2", [P, NT, D], F16)
        hT = sb("hT", [P, FT, N], F32)
        wc = sb("wc", [P, FT, D], F32)
        wvo = sb("wvo", [P, FT, D], F32)
        ohb = sb("ohb", [P, RING, P], F16)
        ohv = sb("ohv", [P, RING, NT * W], F16)
        qT = sb("qT", [P, FT, NA], F32)
        v1 = sb("v1", [P, AT, HEADS, DH + 1], F32)
        qe = sb("qe", [P, 4, AT, M], F32)
        kv = sb("kv", [P, 2, HEADS, DH + 1], F32)
        attn = qe[:, 0:2, :, :].rearrange("p q t m -> p q (t m)")
        attnT = qe[:, 2:4, :, :].rearrange("p q t m -> p (q t) m")
        haT = sb("haT", [P, FT, NA], F32)
        has_in = sb("has_in", [P, CHUNKS[0][1]], F32)

        edst = sb("edst", [EP, EJ], I32)
        esrc = sb("esrc", [EP, EJ], I32)
        tail = r2[0:1, 2848:2848 + 2 * TAILN].bitcast(I32).rearrange("p (k n) -> p k n", k=2)
        iota_i = sb("iota_i", [P, NT * W], I32)
        iota16 = sb("iota16", [P, NT * W], F16)
        thr_i = sb("thr_i", [P, NW], I32)
        thr = sb("thr", [P, NW], F32)
        rowc_i = sb("rowc_i", [P, 4], I32)
        rowc = sb("rowc", [P, 4], F32)
        below = r2[0:EP, 2048:2548].rearrange("p (w j) -> p w j", w=NW)
        nbelow = r2[0:EP, 2560:2610]
        nbelow4 = r2[0:EP, 2624:2824].rearrange("p (w k) -> p w k", w=NW)
        edstf = r2[0:EP, 2832:2842]
        first = sb("first", [P, 2], F32)
        rows = sb("rows", [P, 2], I32)
        g = r2[0:HALF, 0:512].bitcast(I32).rearrange("p (q e) -> p q e", q=2)
        gb_i = r2[0:HALF, 512:768].bitcast(I32).rearrange("p (q e) -> p q e", q=2)
        ga_i = r2[0:HALF, 768:1024].bitcast(I32).rearrange("p (q e) -> p q e", q=2)
        gb = r2[0:HALF, 1024:1280].rearrange("p (q e) -> p q e", q=2)
        gd = r2[0:HALF, 1280:1536].rearrange("p (q e) -> p q e", q=2)
        gx = r2[0:HALF, 1536:1792].rearrange("p (q e) -> p q e", q=2)
        gv = r2[0:HALF, 1792:2048].rearrange("p (q e) -> p q e", q=2)
        nout = sb("nout", [HALF, 1], F32)
        bcol = sb("bcol", [P, NSTEP, 2], F16)
        vcol = sb("vcol", [P, NSTEP, 2], F16)
        fl = sb("fl", [1, 2], F32)
        flag = sb("flag", [1, 1], I32)

        ident = sb("ident", [P, P], F32)
        ones = sb("ones", [P, P], F32)
        c2048 = sb("c2048", [P, P], F16)
        half2 = sb("half2", [P, 2], F32)
        vrow = sb("vrow", [20, P], F32)
        vec = sb("vec", [P, 20], F32)
        pj = sb("pj", [P, 2, 2 * DH], F32)
        pT = sb("pT", [P, M], F32)
        st = sb("st", [P, NT, 6], F32)
        mv = sb("mv", [P, NT, 2], F32)
        lnw = sb("lnw", [P, 4, NT], F32)
        st1 = sb("st1", [P, FT, 3, 6], F32)
        mv1 = sb("mv1", [P, FT, 2], F32)
        bw = sb("bw", [P, 6, FT], F32)
        s1 = sb("s1", [P, FT], F32)
        t1 = sb("t1", [P, FT], F32)
        s2 = sb("s2", [P, FT], F32)
        t2 = sb("t2", [P, FT], F32)
        mxk = sb("mxk", [P, AT, HEADS], F32)
        mxk1 = sb("mxk1", [P, HEADS], F32)
        mk8 = sb("mk8", [HEADS, 1], F32)
        dg8 = sb("dg8", [HEADS, HEADS], F32)
        mxq = sb("mxq", [P, AT, HEADS], F32)
        diag = sb("diag", [P, 2, AT, HEADS], F32)
        kb = sb("kb", [P, AT, HEADS], F32)
        qb = sb("qb", [P, AT, HEADS], F32)
        zz = sb("zz", [P, 4, 4], F32)
        zr = sb("zr", [P, 4, 4], F32)

        si = r2[0:EP, 0:2 * EJ].bitcast(I32).rearrange("p (k j) -> p k j", k=2)
        sa = r2[0:EP, 2 * EJ:3 * EJ]
        sbb = r2[0:EP, 3 * EJ:4 * EJ]
        sd = r2[0:EP, 4 * EJ:5 * EJ]
        sx = r2[0:EP, 5 * EJ:6 * EJ]
        sv = r2[0:EP, 6 * EJ:7 * EJ]
        sw = r2[0:EP, 7 * EJ:8 * EJ]
        wbase = sb("wbase", [EP, 1], F32)
        aw = sb("aw", [P, 2, NT, W], F16)
        zero16 = sb("zero16", [P, NT * W], F16)

        V_G1, V_B1, V_G2, V_B2, V_BC = range(5)

        order = [("first", 6)]
        for i in range(NT):
            order += [(("hT", i), 4 + i % 2)]
            order += {1: [(("q", 0), 2)], 3: [("cols", 7), ("out", 6), (("q", 1), 3)],
                      5: [("vec", 7), ("proj", 6), (("k", 0), 2)], 7: [(("k", 1), 3)]}.get(i, [])
        order += [(("v", i), 4 + i) for i in range(2)]
        order += [("diag", 2)]
        order += [(("uk", i), 3 + i % 4) for i in range(8)]
        order += [("kmaxT", 7), ("kmax", 7)]
        order += [(("uq", i), 3 + i % 4) for i in range(8)]
        order += [(("qfT", h), 2 if h % 2 else 7) for h in range(HEADS)]
        order += [(("agg", 0, FT), 2), (("agg", 0, 0), 7)]
        order += [(("kv", i), 3 + i) for i in range(4)]
        order += [(("attn", i), 3 + i) for i in range(4)]
        order += [(("agg", 0, 1), 3), (("agg", 0, 2), 4)]
        order += [(("attnT", i), 5 + i) for i in range(2)]
        order += [(("ha", i), 5 + i) for i in range(2)]
        agg_banks = iter([2, 7, 3, 4, 5, 6, 2, 7, 3, 0, 1])
        order += [(("agg", c, f), next(agg_banks)) for c in range(3) for f in DEG_FIRST if c or f == 3]
        cycle = [4, 5, 6, 2, 7, 3, 0, 1]
        order_after = [(("conv", c, f), cycle[(c * FT + f) % 8]) for c in range(3) for f in range(FT)]
        order_after += [(("zT", i), cycle[(3 * FT + i) % 8]) for i in range(NT)]
        uses = {}
        nuse = [0] * 8
        for name, b in order + order_after:
            nuse[b] += 1
            uses[name] = (b, nuse[b])
        bank_full = [sem(f"bank_full{b}") for b in range(8)]
        bank_read = [sem(f"bank_read{b}") for b in range(8)]

        def pe_open(pe, name):
            b, n = uses[name]
            if n > 1:
                pe.wait_ge(bank_read[b], n - 1)
            return bank[b]

        def full(name):
            return bank_full[uses[name][0]]

        def read(name):
            return bank_read[uses[name][0]]

        def stored(eng, name):
            b, n = uses[name]
            eng.wait_ge(bank_read[b], n)

        def landed(eng, name):
            b, n = uses[name]
            eng.wait_ge(bank_full[b], n)
            return bank[b]

        x_in = [sem(f"x_in{i}") for i in range(NT)]
        pad_zero = sem("pad_zero")
        dst_in = sem("dst_in")
        src_in = sem("src_in")
        tail_set = sem("tail_set")
        tail_in = sem("tail_in")
        ov_out = sem("ov_out")
        vec_in = sem("vec_in")
        pj_in = sem("pj_in")
        wq_in = sem("wq_in")
        wk_in = sem("wk_in")
        wv_in = sem("wv_in")
        wo_in = sem("wo_in")
        wc_in = sem("wc_in")
        id_set = sem("id_set")
        cst_set = sem("cst_set")
        dve_cst = sem("dve_cst")
        iota_set = sem("iota_set")
        ln_var = sem("ln_var")
        ln_std = sem("ln_std")
        ln_ready = sem("ln_ready")
        h_ready = sem("h_ready")
        h1_ready = sem("h1_ready")
        h_split = sem("h_split")
        rows_ready = sem("rows_ready")
        g_in = [sem(f"g_in{i}") for i in range(2)]
        g_ready = sem("g_ready")
        nb_ready = sem("nb_ready")
        cols_ready = sem("cols_ready")
        flag_ready = sem("flag_ready")
        vec_ready = sem("vec_ready")
        pT_ready = sem("pT_ready")
        hT_ready = sem("hT_ready")
        qk_ready = sem("qk_ready")
        sq_ready = sem("sq_ready")
        v_ready = sem("v_ready")
        uk_copied = sem("uk_copied")
        kmax_part = sem("kmax_part")
        kmax_diag = sem("kmax_diag")
        k_exp = sem("k_exp")
        kf_ready = sem("kf_ready")
        qb_ready = sem("qb_ready")
        q_exp = sem("q_exp")
        qe_used = sem("qe_used")
        qfT_ready = sem("qfT_ready")
        kv_ready = sem("kv_ready")
        attn_ready = sem("attn_ready")
        attnT_ready = sem("attnT_ready")
        haT_ready = sem("haT_ready")
        hTa_ready = sem("hTa_ready")
        bn_var = sem("bn_var")
        bn_std = sem("bn_std")
        oh_ready = sem("oh_ready")
        pair_counted = sem("pair_counted")
        pair_stored = sem("pair_stored")
        sums_final = sem("sums_final")
        mean_ready = sem("mean_ready")
        y_ready = sem("y_ready")
        st2_ready = sem("st2_ready")
        z_act = sem("z_act")
        z_dve = sem("z_dve")
        o_ready = sem("o_ready")
        o_out = sem("o_out")
        s_oh = sem("s_oh")
        s_used = sem("s_used")
        s_link = sem("s_link")
        s_prep = sem("s_prep")
        s_count = sem("s_count")
        s_aw = sem("s_aw")
        s_agg = sem("s_agg")
        s_read = sem("s_read")
        dve_step = sem("dve_step")
        act_step = sem("act_step")
        pool_step = sem("pool_step")

        block = ctx.enter_context(nc.Block())

        @block.sync
        def _(sp):
            sp.dma_start(edst[:, :], dst.rearrange("(p j) -> p j", p=EP)).then_inc(dst_in, 16)
            for i in range(NT):
                n = P if i < NT - 1 else LAST
                if i == NT - 1:
                    sp.wait_ge(pad_zero, 1)
                sp.dma_start(xs[0:n, i, :], x[i * P:i * P + n, :]).then_inc(x_in[i], 16)
                if i == 3:
                    sp.dma_start(wq, w_q.rearrange("(t p) n -> p t n", p=P)).then_inc(wq_in, 16)
                    sp.wait_ge(tail_in, 32)
                    t_ap = tail[:, :, :]
                    for k in range(2):
                        sp.dma_start(edges[FULL:NROW, k * P:(k + 1) * P].rearrange("(o r) e -> o r e", o=1),
                                     bass.AP(t_ap.tensor, t_ap.offset + k * TAILN,
                                             [list(t_ap.ap[0]), [GR, NROW - FULL], [1, P]])).then_inc(ov_out, 16)
            for k, v in enumerate((g1, b1, g2, b2, b_conv)):
                sp.dma_start(vrow[4 * k:4 * k + 4, :], v.rearrange("(t p) -> t p", p=P)).then_inc(vec_in, 16)
            for k in range(2):
                sp.dma_start(pj[:, :, k * DH:(k + 1) * DH], proj.rearrange("(t p) d -> p t d", p=P)).then_inc(pj_in, 16)
            sp.dma_start(wk, w_k.rearrange("(t p) n -> p t n", p=P)).then_inc(wk_in, 16)
            sp.dma_start(wvo[:, :, :], w_v.rearrange("(t p) n -> p t n", p=P)).then_inc(wv_in, 16)
            sp.dma_start(wc[:, :, :], w_conv.rearrange("(t p) n -> p t n", p=P)).then_inc(wc_in, 16)
            for t in range(AT):
                landed(sp, ("v", t))
            sp.dma_start(wvo[:, :, :], w_o.rearrange("(t p) n -> p t n", p=P)).then_inc(wo_in, 16)
            sp.dma_start(esrc[:, :], src.rearrange("(p j) -> p j", p=EP)).then_inc(src_in, 16)
            for i in range(NT):
                n = P if i < NT - 1 else LAST
                sp.wait_ge(o_ready, i + 1)
                sp.dma_start(out[i * P:i * P + n, :], xs[0:n, i, :]).then_inc(o_out, 16)
            sp.wait_ge(src_in, 16)
            sp.wait_ge(o_out, 16 * NT)

        @block.gpsimd
        def _(pool):
            pool.memset(tail[:, :, :], -1).then_inc(tail_set, 1)
            pool.memset(xs[:, NT - 1, :], 0.0).then_inc(pad_zero, 1)
            pool.iota(thr_i[:, :], [[W, NW]], base=0, channel_multiplier=0).then_inc(iota_set, 1)
            pool.iota(rowc_i[:, 0:1], [[0, 1]], base=0, channel_multiplier=1).then_inc(iota_set, 1)
            pool.iota(iota_i[:, :], [[1, NT * W]], base=0, channel_multiplier=0).then_inc(iota_set, 1)
            pool.memset(ident[:, :], 0.0).then_inc(pool_step, 1)
            pool.wait_ge(pool_step, 1)
            pool.affine_select(out=ident[:, :], in_=ident[:, :], compare_op=ALU.not_equal, fill=1.0, base=0,
                               pattern=[[-1, P]], channel_multiplier=1).then_inc(id_set, 1)
            pool.memset(v1[:, :, :, DH:DH + 1], 1.0).then_inc(cst_set, 1)
            pool.memset(c2048[:, :], HSCALE).then_inc(cst_set, 1)
            pool.memset(zero16[:, :], 0.0).then_inc(cst_set, 1)
            pool.memset(half2[:, :], 0.0).then_inc(pool_step, 1)
            pool.wait_ge(pool_step, 2)
            pool.memset(half2[0:DH, 0:1], 0.5).then_inc(cst_set, 1)
            pool.memset(half2[DH:P, 1:2], 0.5).then_inc(cst_set, 1)
            pool.wait_ge(ov_out, 16 * 4)
            pool.wait_ge(rows_ready, 1)
            for hf in range(2):
                pool.indirect_dma_start(out=g[:, hf, :], out_offset=None, in_=edges,
                                        in_offset=bass.IndirectOffsetOnAxis(ap=rows[0:HALF, hf:hf + 1], axis=0),
                                        ).then_inc(g_in[hf], 16)

        @block.scalar
        def _(act):
            for k, e in enumerate((src, dst)):
                act.dma_start(edges[0:FULL, k * P:(k + 1) * P],
                              bass.AP(e.tensor, 0, [[GR, FULL], [1, P]])).then_inc(ov_out, 16)
            act.wait_ge(tail_set, 1)
            for k, e in enumerate((src, dst)):
                act.dma_start(tail[:, k, 0:E - TAIL0], e[TAIL0:E].rearrange("(o n) -> o n", o=1)).then_inc(tail_in, 16)
            def store_hT(i):
                n = P if i < NT - 1 else LAST
                acc = landed(act, ("hT", i))
                act.activation(hT[:, :, i * P:i * P + n], acc[:, :].rearrange("p (t n) -> p t n", t=FT)[:, :, 0:n],
                               ACT.Copy).then_inc(read(("hT", i)), 1)

            stores = [0]

            def store():
                p = stores[0]
                stores[0] += 1
                act.wait_ge(pair_counted, p + 1)
                act.activation(A16[:, :, p * 2 * W:(p + 1) * 2 * W].rearrange("p a (q d) -> p q a d", q=2),
                               bank[p % 2][:, 0:2 * NT * W].rearrange("p (q a d) -> p q a d", q=2, a=NT),
                               ACT.Copy).then_inc(pair_stored, 1)

            def ln_tile(i):
                if i >= 2:
                    act.wait_ge(h_split, i - 1)
                    act.wait_ge(full(("hT", i - 2)), uses[("hT", i - 2)][1])
                act.activation(hring[:, i % 2, :], xs[:, i, :], ACT.Relu,
                               bias=lnw[:, 3, i:i + 1], scale=lnw[:, 2, i:i + 1]).then_inc(h_ready, 1)
                if i not in (0, 2):
                    store_hT(i - 1)
                act.wait_ge(h_ready, i + 1)
                act.activation(h1[:, i, :], hring[:, i % 2, :], ACT.Copy, scale=HSCALE).then_inc(h1_ready, 1)

            def qk(j, i):
                nm, tT = (("q", qT), ("k", kT))[j]
                acc = landed(act, (nm, i))
                act.activation(tT[:, 2 * i:2 * i + 2, :], acc[:, :].rearrange("p (t n) -> p t n", t=2),
                               ACT.Copy, scale=QK_SCALE).then_inc(read((nm, i)), 1)
                stored(act, (nm, i))
                act.activation(sq[:, j, 2 * i:2 * i + 2, :], tT[:, 2 * i:2 * i + 2, :], ACT.Square).then_inc(sq_ready, 1)

            def ln_std_of(gi):
                a, b = LN_GROUPS[gi]
                act.wait_ge(ln_var, gi + 1)
                act.activation(lnw[:, 1, a:b], lnw[:, 0, a:b], ACT.Sqrt).then_inc(ln_std, 1)

            ln_std_of(0)
            act.wait_ge(ln_ready, 1)
            ln_tile(0)
            ln_tile(1)
            store_hT(1)
            ln_std_of(1)
            act.wait_ge(ln_ready, 2)
            ln_tile(2)
            ln_tile(3)
            ln_std_of(2)
            qk(0, 0)
            ln_tile(4)
            ln_tile(5)
            qk(0, 1)
            act.wait_ge(ln_ready, 3)
            ln_tile(6)
            ln_tile(7)
            qk(1, 0)
            store()
            ln_tile(8)
            ln_tile(9)
            store_hT(NT - 1)
            qk(1, 1)
            act.wait_ge(bn_var, 1)
            act.activation(bw[:, 1, :], bw[:, 0, :], ACT.Sqrt).then_inc(bn_std, 1)

            for i in range(3):
                store()
            act.wait_ge(bank_full[uses["cols"][0]], uses["cols"][1])
            for h in range(HEADS):
                acc = landed(act, ("uk", h))
                act.activation(kf[:, :, h, :], acc[:, :].rearrange("p (t m) -> p t m", t=AT),
                               ACT.Copy).then_inc(read(("uk", h)), 1)
                if h in (2, 6):
                    store()
            store()

            def k_exps(t):
                for h in range(HEADS):
                    act.activation(kf[:, t, h, :], kf[:, t, h, :], ACT.Exp, bias=kb[:, t, h:h + 1]).then_inc(k_exp, 1)

            for h in range(HEADS):
                acc = landed(act, ("uq", h))
                act.wait_ge(qb_ready, h + 1)
                if h >= 4:
                    act.wait_ge(full(("qfT", h - 4)), uses[("qfT", h - 4)][1])
                act.activation(qe[:, h % 4, 0, :], acc[:, 0:M], ACT.Exp, bias=qb[:, 0, h:h + 1])
                act.activation(qe[:, h % 4, 1, :], acc[:, M:2 * M], ACT.Exp, bias=qb[:, 1, h:h + 1]).then_inc(read(("uq", h)), 1)
                if h == 1:
                    stored(act, "kmax")
                    k_exps(0)
                if h == 3:
                    k_exps(1)
                if h % 2:
                    store()

            while stores[0] < NPAIR:
                store()

            for c, (c0, cn) in enumerate(CHUNKS):
                for f in range(FT):
                    acc = landed(act, ("conv", c, f))
                    act.activation(yT[:, f, c0:c0 + cn], acc[:, 0:cn], ACT.Relu,
                                   bias=vec[:, 4 * V_BC + f:4 * V_BC + f + 1]).then_inc(read(("conv", c, f)), 1)
            act.wait_ge(bn_var, 2)
            act.activation(bw[:, 1, :], bw[:, 0, :], ACT.Sqrt).then_inc(bn_std, 1)
            act.wait_ge(st2_ready, 1)
            for c, f in Z_ACT:
                c0, cn = ZC[c]
                act.activation(yT[:, f, c0:c0 + cn], yT[:, f, c0:c0 + cn], ACT.Identity,
                               bias=t2[:, f:f + 1], scale=s2[:, f:f + 1]).then_inc(z_act, 1)

        @block.tensor
        def _(pe):
            pe.wait_ge(id_set, 1)
            pe.wait_ge(dve_cst, 1)
            pe.wait_ge(nb_ready, 1)
            acc = pe_open(pe, "first")
            for hf in range(2):
                last = nc.tensor.matmul(acc[0:HALF, hf:hf + 1],
                                        nbelow4[:, hf * NW // 2:(hf + 1) * NW // 2, :].rearrange("p w k -> p (w k)"),
                                        ones[0:EP, 0:1], start=True, stop=True)
            last.then_inc(full("first"), 1)
            def transpose_h(i):
                pe.wait_ge(h_ready, i + 1)
                acc = pe_open(pe, ("hT", i))
                for f in range(FT):
                    last = nc.tensor.transpose(acc[:, f * P:(f + 1) * P], hring[:, i % 2, f * P:(f + 1) * P], ident[:, :])
                last.then_inc(full(("hT", i)), 1)

            def qk(nm, w, i):
                acc = pe_open(pe, (nm, i))
                for t in range(2):
                    c = (2 * i + t) * P
                    for f in range(FT):
                        last = nc.tensor.matmul(acc[:, t * NA:(t + 1) * NA], w[:, f, c:c + P], hT[:, f, 0:NA],
                                                start=(f == 0), stop=(f == FT - 1))
                last.then_inc(full((nm, i)), 1)

            counts = [0]

            def count():
                p = counts[0]
                counts[0] += 1
                pe.wait_ge(oh_ready, p + 1)
                if p >= 2:
                    pe.wait_ge(pair_stored, p - 1)
                for q in range(2):
                    for k in range(K):
                        s = (2 * (p % 2) + q) * K + k
                        last = nc.tensor.matmul(bank[p % 2][:, q * NT * W:(q + 1) * NT * W], ohb[:, s, :], ohv[:, s, :],
                                                start=(k == 0), stop=(k == K - 1))
                last.then_inc(pair_counted, 1)

            transpose_h(0)
            transpose_h(1)
            for i in range(2):
                stored(pe, ("hT", i))
            pe.wait_ge(wq_in, 16)
            qk("q", wq, 0)
            transpose_h(2)
            transpose_h(3)
            pe.wait_ge(g_ready, 1)
            acc = pe_open(pe, "cols")
            for j, m in enumerate((gb, gv)):
                for hf in range(2):
                    o = (2 * j + hf) * HALF
                    last = nc.tensor.transpose(acc[:, o:o + HALF], m[:, hf, :], ident[0:HALF, 0:HALF])
            last.then_inc(full("cols"), 1)
            acc = pe_open(pe, "out")
            nc.tensor.matmul(acc[0:1, 0:1], nout[:, 0:1], ones[0:HALF, 0:1], start=True, stop=True).then_inc(full("out"), 1)
            qk("q", wq, 1)
            transpose_h(4)
            transpose_h(5)
            pe.wait_ge(vec_in, 16 * 5)
            acc = pe_open(pe, "vec")
            nc.tensor.transpose(acc[:, 0:20], vrow[:, :], ident[0:20, 0:20]).then_inc(full("vec"), 1)
            pe.wait_ge(pj_in, 32)
            acc = pe_open(pe, "proj")
            for t in range(2):
                last = nc.tensor.transpose(acc[:, t * P:(t + 1) * P], pj[:, t, :], ident[:, :])
            last.then_inc(full("proj"), 1)
            pe.wait_ge(wk_in, 16)
            qk("k", wk, 0)
            count()
            for i in range(6, NT):
                transpose_h(i)
                if i == 7:
                    qk("k", wk, 1)
                    count()

            def aggregate(c, f):
                c0, cn = CHUNKS[c]
                pe.wait_ge(pair_stored, -(-(c0 + cn) // (2 * W)))
                pe.wait_ge(h_split, NT)
                acc = pe_open(pe, ("agg", c, f))
                for s in range(NT):
                    for hh in (h1, h2) if f < FT else (c2048,):
                        lhs = hh[:, s, f * P:(f + 1) * P] if f < FT else c2048[:, :]
                        last = nc.tensor.matmul(acc[:, 0:cn], lhs, A16[:, s, c0:c0 + cn],
                                                start=(s == 0 and hh is not h2), stop=(s == NT - 1 and hh is not h1))
                last.then_inc(full(("agg", c, f)), 1)

            pe.wait_ge(wv_in, 16)
            for t in range(AT):
                acc = pe_open(pe, ("v", t))
                for f in range(FT):
                    last = nc.tensor.matmul(acc[:, :], hT[:, f, t * P:(t + 1) * P], wvo[:, f, :],
                                            start=(f == 0), stop=(f == FT - 1))
                last.then_inc(full(("v", t)), 1)
                count()
            def diagonal(j, t):
                if (j, t) == (0, 0):
                    pe.wait_ge(sq_ready, 4)
                    pe.wait_ge(cst_set, 5)
                    pe_open(pe, "diag")
                acc = bank[uses["diag"][0]]
                for c in range(FT):
                    o = (j * AT + t) * HEADS + 2 * c
                    last = nc.tensor.matmul(acc[:, o:o + 2], sq[:, j, c, t * P:(t + 1) * P], half2[:, :],
                                            start=True, stop=True)
                if (j, t) == (1, 1):
                    last.then_inc(full("diag"), 1)

            def features(nm, tT, h):
                p0 = h % 2 * DH
                acc = pe_open(pe, (nm, h))
                for t in range(AT):
                    last = nc.tensor.matmul(acc[:, t * M:(t + 1) * M], tT[p0:p0 + DH, h // 2, t * P:(t + 1) * P],
                                            pT[p0:p0 + DH, :], start=True, stop=True)
                last.then_inc(full((nm, h)), 1)

            def transpose_qf(h):
                acc = pe_open(pe, ("qfT", h))
                stored(pe, ("uq", h))
                for m in range(2):
                    for t in range(2):
                        o = (2 * m + t) * P
                        last = nc.tensor.transpose(acc[:, o:o + P], qe[:, h % 4, t, m * P:(m + 1) * P], ident[:, :])
                last.then_inc(full(("qfT", h)), 1)

            stored(pe, "proj")
            for i in range(8):
                features("uk", kT, i)
                if i < 4:
                    diagonal(i // 2, i % 2)
                if i in (1, 5):
                    count()
            pe.wait_ge(kmax_part, 1)
            acc = pe_open(pe, "kmaxT")
            nc.tensor.transpose(acc[0:HEADS, 0:P], mxk1[:, :], ident[:, :]).then_inc(full("kmaxT"), 1)
            count()
            pe.wait_ge(kmax_diag, 1)
            acc = pe_open(pe, "kmax")
            nc.tensor.matmul(acc[:, 0:HEADS], ones[0:HEADS, :], dg8[:, :], start=True, stop=True).then_inc(full("kmax"), 1)
            for i in range(4):
                features("uq", qT, i)
                if i % 2:
                    count()
            for hp in range(4):
                transpose_qf(2 * hp)
                transpose_qf(2 * hp + 1)
                if hp < 2:
                    features("uq", qT, 2 * hp + 4)
                    features("uq", qT, 2 * hp + 5)
                count()

            aggregate(0, FT)
            aggregate(0, 0)
            for i in range(4):
                m, half = divmod(i, 2)
                acc = pe_open(pe, ("kv", i))
                pe.wait_ge(kf_ready, 2)
                stored(pe, ("v", 0))
                stored(pe, ("v", 1))
                for j in range(4):
                    h = 4 * half + j
                    for t in range(AT):
                        last = nc.tensor.matmul(acc[:, j * (DH + 1):(j + 1) * (DH + 1)], kf[:, t, h, m * P:(m + 1) * P],
                                                v1[:, t, h, :], start=(t == 0), stop=(t == AT - 1))
                last.then_inc(full(("kv", i)), 1)
                count()
            for h in range(HEADS):
                stored(pe, ("qfT", h))
            for i in range(4):
                stored(pe, ("kv", i))
            for i in range(4):
                t, half = divmod(i, 2)
                acc = pe_open(pe, ("attn", i))
                for j in range(4):
                    h = 4 * half + j
                    for m in range(2):
                        last = nc.tensor.matmul(acc[:, j * (DH + 1):(j + 1) * (DH + 1)], qfT[:, m, h, t * P:(t + 1) * P],
                                                kv[:, m, h, :], start=(m == 0), stop=(m == 1))
                last.then_inc(full(("attn", i)), 1)
                if i % 2:
                    count()
            aggregate(0, 1)
            for i in range(4):
                stored(pe, ("attn", i))
            for i in range(2):
                acc = pe_open(pe, ("attnT", i))
                for c in range(2):
                    for t in range(AT):
                        o = (2 * c + t) * P
                        last = nc.tensor.transpose(acc[:, o:o + P], attn[:, t, (2 * i + c) * P:(2 * i + c + 1) * P], ident[:, :])
                last.then_inc(full(("attnT", i)), 1)
            count()
            aggregate(0, 2)
            pe.wait_ge(wo_in, 16)
            for i in range(2):
                stored(pe, ("attnT", i))
            for i in range(2):
                acc = pe_open(pe, ("ha", i))
                for t in range(2):
                    o = (2 * i + t) * P
                    for c in range(FT):
                        last = nc.tensor.matmul(acc[:, t * NA:(t + 1) * NA], wvo[:, c, o:o + P], attnT[:, c, :],
                                                start=(c == 0), stop=(c == FT - 1))
                last.then_inc(full(("ha", i)), 1)
            count()

            aggregate(0, 3)
            for f in DEG_FIRST:
                aggregate(1, f)
                if f != 3:
                    count()
            for f in DEG_FIRST:
                aggregate(2, f)

            pe.wait_ge(flag_ready, 1)
            covered = pe.value_load(flag[0:1, 0:1], min_val=0, max_val=1)
            with pe.If(covered == 0):
                for c in range(3):
                    for f in DEG_FIRST:
                        stored(pe, ("agg", c, f))
                with pe.Fori(0, NW) as w:
                    nc.tensor.matmul(bank[0][:, 0:NT * W], zero16[:, 0:P], zero16[:, :], start=True, stop=False)
                    with pe.Fori(0, EJ // 8) as gg:
                        pe.wait_ge(s_oh, w * (EJ // 8) + gg + 1)
                        for s in range(8):
                            last = nc.tensor.matmul(bank[0][:, 0:NT * W], ohb[0:EP, s, :], ohv[0:EP, s, :],
                                                    start=False, stop=False)
                        last.then_inc(s_used, 1)
                    nc.tensor.matmul(bank[0][:, 0:NT * W], zero16[:, 0:P], zero16[:, :], start=False, stop=True).then_inc(s_count, 1)
                    pe.wait_ge(s_aw, w + 1)
                    for f in range(FT + 1):
                        for s in range(NT):
                            for hl in range(2):
                                for hh in (h1, h2) if f < FT else (c2048,):
                                    lhs = hh[:, s, f * P:(f + 1) * P] if f < FT else c2048[:, :]
                                    last = nc.tensor.matmul(bank[2 + f][:, 0:W], lhs, aw[:, hl, s, :],
                                                            start=(s == 0 and hl == 0 and hh is not h2),
                                                            stop=(s == NT - 1 and hl == 1 and hh is not h1))
                    last.then_inc(s_agg, 1)
                    pe.wait_ge(s_read, w + 1)

            pe.wait_ge(wc_in, 16)
            pe.wait_ge(sums_final, 1)
            for c, (c0, cn) in enumerate(CHUNKS):
                pe.wait_ge(mean_ready, FT * (c + 1))
                for o in range(FT):
                    acc = pe_open(pe, ("conv", c, o))
                    for f in range(FT):
                        last = nc.tensor.matmul(acc[:, 0:cn], wc[:, f, o * P:(o + 1) * P], aggT[:, f, c0:c0 + cn],
                                         start=(f == 0), stop=(f == FT - 1))
                    last.then_inc(full(("conv", c, o)), 1)
            for i in range(NT):
                n = P if i < NT - 1 else LAST
                c = i * P // 512
                pe.wait_ge(z_dve, sum(1 for cc, _ in Z_DVE if cc <= c))
                pe.wait_ge(z_act, sum(1 for cc, _ in Z_ACT if cc <= c))
                if i < 8:
                    acc = pe_open(pe, ("zT", i))
                else:
                    pe.wait_ge(o_ready, i - 7)
                    acc = bank[uses[("zT", i)][0]]
                for f in range(FT):
                    last = nc.tensor.transpose(acc[0:n, f * P:(f + 1) * P], yT[:, f, i * P:i * P + n], ident[:, :])
                last.then_inc(full(("zT", i)), 1)

        @block.vector
        def _(dve):
            V = nc.vector
            step = [0]

            def link(ins):
                step[0] += 1
                ins.then_inc(dve_step, 1)
                dve.wait_ge(dve_step, step[0])

            def rstd(var, std, r, t):
                link(V.reciprocal(r, std))
                link(V.tensor_tensor(t, r, r, ALU.mult))
                link(V.tensor_tensor(t, t, var, ALU.mult))
                link(V.tensor_scalar(t, t, -0.5, 1.5, ALU.mult, ALU.add))
                link(V.tensor_tensor(r, r, t, ALU.mult))

            V.memset(ones[:, :], 1.0).then_inc(dve_cst, 1)
            dve.wait_ge(iota_set, 3)
            link(V.tensor_copy(thr[:, :], thr_i[:, :]))
            link(V.tensor_copy(iota16[:, :], iota_i[:, :]))
            link(V.tensor_scalar(rowc_i[:, 1:2], rowc_i[:, 0:1], K - 1, None, ALU.bitwise_and))
            link(V.tensor_scalar(rowc_i[:, 2:3], rowc_i[:, 0:1], 2, None, ALU.arith_shift_right))
            link(V.tensor_scalar(rowc[:, 0:1], rowc_i[:, 1:2], float(P // GR), None, ALU.mult))
            link(V.tensor_scalar(rowc[:, 1:2], rowc_i[:, 2:3], float(W), None, ALU.mult))
            link(V.tensor_scalar(rowc[:, 2:3], rowc[:, 1:2], float(W * NW // 2), None, ALU.add))
            dve.wait_ge(dst_in, 16)
            link(V.tensor_copy(edstf[:, :], edst[:, ::GR]))
            nj = EJ // GR
            link(V.tensor_tensor(below[:, :, :], edstf[:, :].unsqueeze(1).to_broadcast([EP, NW, nj]),
                                 thr[0:EP, :].unsqueeze(2).to_broadcast([EP, NW, nj]), ALU.is_lt))
            link(V.tensor_reduce(nbelow[:, :], below[:, :, :], AX_X, ALU.add))
            V.tensor_copy(nbelow4[:, :, :], nbelow[:, :].unsqueeze(2).to_broadcast([EP, NW, K])).then_inc(nb_ready, 1)

            def ln_stats(gi):
                a, b = LN_GROUPS[gi]
                for i in range(a, b):
                    if i == NT - 1:
                        dve.wait_ge(pad_zero, 1)
                    dve.wait_ge(x_in[i], 16)
                    ins = V.bn_stats(st[:, i, :], xs[:, i, :])
                link(ins)
                for i in range(a, b):
                    ins = V.bn_aggr(mv[:, i, :], st[:, i, :])
                link(ins)
                V.tensor_scalar(lnw[:, 0, a:b], mv[:, a:b, 1], EPS, None, ALU.add).then_inc(ln_var, 1)

            def ln_scale(gi):
                a, b = LN_GROUPS[gi]
                dve.wait_ge(ln_std, gi + 1)
                rstd(lnw[:, 0, a:b], lnw[:, 1, a:b], lnw[:, 2, a:b], lnw[:, 3, a:b])
                V.scalar_tensor_tensor(out=lnw[:, 3, a:b], in0=mv[:, a:b, 0], scalar=-1.0, in1=lnw[:, 2, a:b],
                                       op0=ALU.mult, op1=ALU.mult).then_inc(ln_ready, 1)

            def split(i):
                dve.wait_ge(h1_ready, i + 1)
                V.scalar_tensor_tensor(out=h2[:, i, :], in0=hring[:, i % 2, :], scalar=HSCALE, in1=h1[:, i, :],
                                       op0=ALU.mult, op1=ALU.subtract).then_inc(h_split, 1)

            def bn_piece(c):
                for i in range(4 * c, min(4 * c + 4, NT)):
                    stored(dve, ("hT", i))
                for f in range(FT):
                    ins = V.bn_stats(st1[:, f, c, :], hT[:, f, c * 512:min((c + 1) * 512, N)])
                if c == 2:
                    link(ins)

            pairs = [0]

            def one_hots():
                p = pairs[0]
                pairs[0] += 1
                if p >= 2:
                    dve.wait_ge(pair_counted, p - 1)
                n = 2 * K
                s0 = p % 2 * n
                for oh, col, size in ((ohb, bcol, P), (ohv, vcol, NT * W)):
                    shape = [P, n, size // 2, 2]
                    last = V.tensor_tensor(oh[:, s0:s0 + n, :].rearrange("p s (m t) -> p s m t", t=2),
                                           iota16[:, 0:size].rearrange("p (m t) -> p m t", t=2).unsqueeze(1).to_broadcast(shape),
                                           col[:, p * n:(p + 1) * n, :].unsqueeze(2).to_broadcast(shape), ALU.is_equal)
                last.then_inc(oh_ready, 1)

            dve.wait_ge(full("first"), uses["first"][1])
            V.tensor_scalar(first[0:HALF, :], bank[uses["first"][0]][0:HALF, 0:2], -1.0, 0.0, ALU.add, ALU.max
                            ).then_inc(read("first"), 1)
            stored(dve, "first")
            V.tensor_scalar(rows[0:HALF, :], first[0:HALF, :], rowc[0:HALF, 0:1], None, ALU.add).then_inc(rows_ready, 1)
            ln_stats(0)
            ln_scale(0)
            ln_stats(1)
            split(0)
            split(1)
            ln_scale(1)
            ln_stats(2)
            split(2)
            for hf in range(2):
                dve.wait_ge(g_in[hf], 16)
            link(V.tensor_scalar(gb_i[:, :, :], g[:, :, 0:P], P - 1, None, ALU.bitwise_and))
            link(V.tensor_scalar(ga_i[:, :, :], g[:, :, 0:P], 7, None, ALU.arith_shift_right))
            for hf in range(2):
                link(V.tensor_scalar(gd[:, hf, :], g[:, hf, P:2 * P], rowc[0:HALF, 1 + hf:2 + hf], None, ALU.subtract))
            link(V.tensor_copy(gb[:, :, :], gb_i[:, :, :]))
            link(V.tensor_scalar(gx[:, :, :], gd[:, :, :], 0.0, None, ALU.is_lt))
            link(V.scalar_tensor_tensor(out=gx[:, :, :], in0=gd[:, :, :], scalar=W - 0.5, in1=gx[:, :, :],
                                        op0=ALU.is_gt, op1=ALU.add))
            link(V.scalar_tensor_tensor(out=gv[:, :, :], in0=ga_i[:, :, :], scalar=float(W), in1=gd[:, :, :],
                                        op0=ALU.mult, op1=ALU.add))
            link(V.tensor_scalar(gx[:, :, :], gx[:, :, :], 0.5, None, ALU.is_gt, ALU.add, accum_out=nout[:, :]))
            V.scalar_tensor_tensor(out=gv[:, :, :], in0=gx[:, :, :], scalar=4096.0, in1=gv[:, :, :],
                                   op0=ALU.mult, op1=ALU.add).then_inc(g_ready, 1)

            split(3)
            ln_scale(2)
            split(4)
            dve.wait_ge(full("cols"), uses["cols"][1])
            acc = bank[uses["cols"][0]]
            V.tensor_copy(bcol[:, :, :], acc[:, 0:NSTEP].unsqueeze(2).to_broadcast([P, NSTEP, 2]))
            V.tensor_copy(vcol[:, :, :], acc[:, NSTEP:2 * NSTEP].unsqueeze(2).to_broadcast([P, NSTEP, 2])
                          ).then_inc(read("cols"), 1)
            stored(dve, "cols")
            dve.wait_ge(full("out"), uses["out"][1])
            V.tensor_scalar(fl[0:1, 1:2], bank[uses["out"][0]][0:1, 0:1], float(NSTEP * P - E), None, ALU.is_equal
                            ).then_inc(read("out"), 1)
            stored(dve, "out")
            V.tensor_copy(flag[:, :], fl[0:1, 1:2]).then_inc(flag_ready, 1)
            one_hots()
            landed(dve, "vec")
            V.tensor_copy(vec[:, :], bank[uses["vec"][0]][:, 0:20]).then_inc(read("vec"), 1)
            landed(dve, "proj")
            V.tensor_copy(pT[:, :], bank[uses["proj"][0]][:, 0:M]).then_inc(read("proj"), 1)
            split(5)
            split(6)
            one_hots()
            bn_piece(0)
            split(7)
            split(8)
            bn_piece(1)
            split(9)
            one_hots()
            bn_piece(2)
            for f in range(FT):
                ins = V.bn_aggr(mv1[:, f, :], st1[:, f, :, :].rearrange("p c s -> p (c s)"))
            link(ins)
            link(V.tensor_scalar(bw[:, 0, :], mv1[:, :, 1], EPS, None, ALU.add))
            V.tensor_scalar(bw[:, 4, :], mv1[:, :, 1], EPS, None, ALU.add).then_inc(bn_var, 1)
            one_hots()

            for t in range(AT):
                acc = landed(dve, ("v", t))
                dve.wait_ge(cst_set, 5)
                V.tensor_copy(v1[:, t, :, 0:DH], acc[:, :].rearrange("p (h d) -> p h d", h=HEADS)).then_inc(read(("v", t)), 1)
                one_hots()

            dve.wait_ge(bn_std, 1)
            rstd(bw[:, 0, :], bw[:, 1, :], bw[:, 2, :], bw[:, 3, :])
            link(V.tensor_tensor(s1[:, :], vec[:, 4 * V_G1:4 * V_G1 + 4], bw[:, 2, :], ALU.mult))
            link(V.tensor_tensor(bw[:, 3, :], mv1[:, :, 0], s1[:, :], ALU.mult))
            link(V.tensor_tensor(t1[:, :], vec[:, 4 * V_B1:4 * V_B1 + 4], bw[:, 3, :], ALU.subtract))

            for h in range(HEADS):
                stored(dve, ("uk", h))
                ins = V.tensor_reduce(mxk[:, :, h], kf[:, :, h, :], AX_X, ALU.max)
                if h in (1, 5):
                    one_hots()
                if h == 4:
                    acc = landed(dve, "diag")
                    V.tensor_copy(diag[:, :, :, :].rearrange("p j t h -> p (j t h)"), acc[:, 0:32]).then_inc(read("diag"), 1)
                    stored(dve, "diag")
            link(ins)
            V.tensor_tensor(mxk1[:, :], mxk[:, 0, :], mxk[:, 1, :], ALU.max).then_inc(kmax_part, 1)
            acc = landed(dve, "kmaxT")
            V.tensor_reduce(mk8[:, :], acc[0:HEADS, 0:P], AX_X, ALU.max).then_inc(read("kmaxT"), 1)
            stored(dve, "kmaxT")
            V.tensor_scalar(dg8[:, :], ident[0:HEADS, 0:HEADS], mk8[:, 0:1], None, ALU.mult).then_inc(kmax_diag, 1)

            acc = landed(dve, "kmax")
            for t in range(AT):
                ins = V.scalar_tensor_tensor(out=kb[:, t, :], in0=acc[:, 0:HEADS], scalar=-1.0, in1=diag[:, 1, t, :],
                                             op0=ALU.mult, op1=ALU.subtract)
            ins.then_inc(read("kmax"), 1)
            one_hots()

            def in_degrees(c):
                c0, cn = CHUNKS[c]
                acc = landed(dve, ("agg", c, FT))
                link(V.tensor_scalar(rdeg[:, c0:c0 + cn], acc[:, 0:cn], HSCALE, None, ALU.max))
                V.tensor_scalar(has_in[:, 0:cn], acc[:, 0:cn], 1.0, None, ALU.min).then_inc(read(("agg", c, FT)), 1)
                link(V.reciprocal(rdeg[:, c0:c0 + cn], rdeg[:, c0:c0 + cn]))

            def mean(c, f):
                c0, cn = CHUNKS[c]
                acc = landed(dve, ("agg", c, f))
                V.scalar_tensor_tensor(out=aggT[:, f, c0:c0 + cn], in0=acc[:, 0:cn], scalar=s1[:, f:f + 1],
                                       in1=rdeg[:, c0:c0 + cn], op0=ALU.mult, op1=ALU.mult).then_inc(read(("agg", c, f)), 1)
                stored(dve, ("agg", c, f))
                V.scalar_tensor_tensor(out=aggT[:, f, c0:c0 + cn], in0=has_in[:, 0:cn], scalar=t1[:, f:f + 1],
                                       in1=aggT[:, f, c0:c0 + cn], op0=ALU.mult, op1=ALU.add).then_inc(mean_ready, 1)

            def q_bias(h):
                acc = landed(dve, ("uq", h))
                link(V.tensor_reduce(mxq[:, :, h], acc[:, :].rearrange("p (t m) -> p t m", t=AT), AX_X, ALU.max))
                V.scalar_tensor_tensor(out=qb[:, :, h], in0=mxq[:, :, h], scalar=-1.0,
                                       in1=diag[:, 0, :, h], op0=ALU.mult, op1=ALU.subtract).then_inc(qb_ready, 1)

            def q_feat(h):
                acc = landed(dve, ("qfT", h))
                if h == 0:
                    landed(dve, ("k", 1))
                V.tensor_scalar(qfT[:, :, h, :], acc[:, :].rearrange("p (m n) -> p m n", m=2), PHI_SCALE, KEPS,
                                ALU.mult, ALU.add).then_inc(read(("qfT", h)), 1)

            for i in range(4):
                q_bias(i)
                if i % 2:
                    one_hots()
            for hp in range(4):
                q_feat(2 * hp)
                q_feat(2 * hp + 1)
                if hp < 2:
                    q_bias(2 * hp + 4)
                    q_bias(2 * hp + 5)
                else:
                    t = hp - 2
                    dve.wait_ge(k_exp, HEADS * (t + 1))
                    V.tensor_scalar(kf[:, t, :, :], kf[:, t, :, :], PHI_SCALE, KEPS, ALU.mult, ALU.add).then_inc(kf_ready, 1)
                one_hots()
            for i in range(4):
                m, half = divmod(i, 2)
                acc = landed(dve, ("kv", i))
                V.tensor_copy(kv[:, m, 4 * half:4 * half + 4, :], acc[:, 0:4 * (DH + 1)].rearrange("p (h d) -> p h d", h=4)
                              ).then_inc(read(("kv", i)), 1)
                one_hots()
            for i in range(4):
                t, half = divmod(i, 2)
                acc = landed(dve, ("attn", i))
                a = acc[:, 0:4 * (DH + 1)].rearrange("p (h d) -> p h d", h=4)
                link(V.tensor_scalar(zz[:, i, :], a[:, :, DH], KEPS, None, ALU.add))
                link(V.reciprocal(zr[:, i, :], zz[:, i, :]))
                V.tensor_tensor(attn[:, t, half * 256:(half + 1) * 256].rearrange("p (h d) -> p h d", h=4), a[:, :, 0:DH],
                                zr[:, i, :].unsqueeze(2).to_broadcast([P, 4, DH]), ALU.mult).then_inc(read(("attn", i)), 1)
                if i % 2:
                    one_hots()
            in_degrees(0)
            mean(0, 0)
            for i in range(2):
                acc = landed(dve, ("attnT", i))
                V.tensor_copy(attnT[:, 2 * i:2 * i + 2, :], acc[:, :].rearrange("p (t n) -> p t n", t=2)
                              ).then_inc(read(("attnT", i)), 1)
            one_hots()
            mean(0, 1)
            for i in range(2):
                acc = landed(dve, ("ha", i))
                V.tensor_copy(haT[:, 2 * i:2 * i + 2, :], acc[:, :].rearrange("p (t n) -> p t n", t=2)
                              ).then_inc(read(("ha", i)), 1)
                stored(dve, ("ha", i))
            V.tensor_tensor(hT[:, :, 0:NA], hT[:, :, 0:NA], haT[:, :, :], ALU.add).then_inc(hTa_ready, 1)

            dve.wait_ge(hTa_ready, 1)
            one_hots()
            mean(0, 2)
            mean(0, 3)
            in_degrees(1)
            one_hots()
            for f in range(FT):
                mean(1, f)
                if f == 0:
                    one_hots()
            covered = dve.value_load(flag[0:1, 0:1], min_val=0, max_val=1)
            links = step[0]
            with dve.If(covered == 1):
                V.memset(fl[0:1, 0:1], 0.0).then_inc(sums_final, 1)
                in_degrees(2)
                for f in range(FT):
                    mean(2, f)
            with dve.Else():
                step[0] = links
                in_degrees(2)
                for f in range(FT):
                    mean(2, f)
                nprep = [0]

                def prep(ins):
                    nprep[0] += 1
                    ins.then_inc(s_prep, 1)
                    dve.wait_ge(s_prep, nprep[0])

                dve.wait_ge(src_in, 16)
                prep(V.tensor_scalar(si[:, 0, :], esrc[:, :], 7, None, ALU.arith_shift_right))
                prep(V.tensor_scalar(si[:, 1, :], esrc[:, :], P - 1, None, ALU.bitwise_and))
                prep(V.tensor_copy(sa[:, :], si[:, 0, :]))
                prep(V.tensor_copy(sbb[:, :], si[:, 1, :]))
                prep(V.tensor_copy(sd[:, :], edst[:, :]))
                prep(V.memset(wbase[:, :], 0.0))
                V.memset(fl[0:1, 0:1], 0.0).then_inc(s_used, 1)
                with dve.Fori(0, NW) as w:
                    seq = [0]

                    def chain(ins):
                        seq[0] += 1
                        ins.then_inc(s_link, 1)
                        dve.wait_ge(s_link, w * SLOW_LINKS + seq[0])

                    chain(V.tensor_scalar(sx[:, :], sd[:, :], wbase[:, 0:1], None, ALU.subtract))
                    chain(V.scalar_tensor_tensor(out=sv[:, :], in0=sa[:, :], scalar=float(W), in1=sx[:, :],
                                                 op0=ALU.mult, op1=ALU.add))
                    chain(V.tensor_scalar(sw[:, :], sx[:, :], 0.0, None, ALU.is_lt))
                    chain(V.scalar_tensor_tensor(out=sx[:, :], in0=sx[:, :], scalar=W - 0.5, in1=sw[:, :],
                                                 op0=ALU.is_gt, op1=ALU.add))
                    chain(V.tensor_scalar(sx[:, :], sx[:, :], 4096.0, None, ALU.mult))
                    chain(V.tensor_tensor(sv[:, :], sv[:, :], sx[:, :], ALU.add))
                    seq[0] += 1
                    V.tensor_scalar(wbase[:, :], wbase[:, :], float(W), None, ALU.add).then_inc(s_link, 1)
                    with dve.Fori(0, EJ // 8) as gg:
                        dve.wait_ge(s_used, w * (EJ // 8) + gg + 1)
                        for s in range(8):
                            V.tensor_scalar(ohb[0:EP, s, :], iota16[0:EP, 0:P], sbb[:, ds(8 * gg + s, 1)], None, ALU.is_equal)
                            last = V.tensor_scalar(ohv[0:EP, s, :], iota16[0:EP, :], sv[:, ds(8 * gg + s, 1)], None, ALU.is_equal)
                        last.then_inc(s_oh, 1)
                    dve.wait_ge(s_count, w + 1)
                    cnt = bank[0][:, 0:NT * W].rearrange("p (a d) -> p a d", a=NT)
                    chain(V.tensor_copy(aw[:, 0, :, :], cnt))
                    V.tensor_tensor(aw[:, 1, :, :], cnt, aw[:, 0, :, :], ALU.subtract).then_inc(s_aw, 1)
                    dve.wait_ge(s_agg, w + 1)
                    for f in range(FT):
                        V.tensor_copy(aggT[:, f, ds(W * w, W)], bank[2 + f][:, 0:W])
                    V.tensor_copy(deg[:, ds(W * w, W)], bank[6][:, 0:W]).then_inc(s_read, 1)
                prep(V.memset(fl[0:1, 0:1], 0.0))
                prep(V.tensor_scalar(rdeg, deg, HSCALE, None, ALU.max))
                prep(V.reciprocal(rdeg, rdeg))
                for c0, cn in CHUNKS:
                    prep(V.tensor_scalar(has_in[:, 0:cn], deg[:, c0:c0 + cn], 1.0, None, ALU.min))
                    for f in range(FT):
                        prep(V.scalar_tensor_tensor(out=aggT[:, f, c0:c0 + cn], in0=aggT[:, f, c0:c0 + cn], scalar=s1[:, f:f + 1],
                                                    in1=rdeg[:, c0:c0 + cn], op0=ALU.mult, op1=ALU.mult))
                        prep(V.scalar_tensor_tensor(out=aggT[:, f, c0:c0 + cn], in0=has_in[:, 0:cn], scalar=t1[:, f:f + 1],
                                                    in1=aggT[:, f, c0:c0 + cn], op0=ALU.mult, op1=ALU.add))
                V.memset(fl[0:1, 0:1], 0.0).then_inc(sums_final, 1)

            ny = [0]

            def add_y(c):
                c0, cn = CHUNKS[c]
                for f in range(FT):
                    stored(dve, ("conv", c, f))
                    own = max(0, min(NA - c0, cn))
                    if own:
                        ins = V.tensor_tensor(yT[:, f, c0:c0 + own], yT[:, f, c0:c0 + own], hT[:, f, c0:c0 + own], ALU.add)
                    ins = V.scalar_tensor_tensor(out=yT[:, f, c0 + own:c0 + cn], in0=hT[:, f, c0 + own:c0 + cn],
                                                 scalar=haT[:, f, NA - 1:NA], in1=yT[:, f, c0 + own:c0 + cn],
                                                 op0=ALU.add, op1=ALU.add)
                    ny[0] += 1
                    ins.then_inc(y_ready, 1)
                    dve.wait_ge(y_ready, ny[0])
                    ins = V.bn_stats(st1[:, f, c, :], yT[:, f, c0:c0 + cn])
                return ins

            add_y(0)
            add_y(1)
            link(add_y(2))
            for f in range(FT):
                ins = V.bn_aggr(mv1[:, f, :], st1[:, f, :, :].rearrange("p c s -> p (c s)"))
            link(ins)
            V.tensor_scalar(bw[:, 0, :], mv1[:, :, 1], EPS, None, ALU.add).then_inc(bn_var, 1)
            dve.wait_ge(bn_std, 2)
            rstd(bw[:, 0, :], bw[:, 1, :], bw[:, 2, :], bw[:, 3, :])
            link(V.tensor_tensor(s2[:, :], vec[:, 4 * V_G2:4 * V_G2 + 4], bw[:, 2, :], ALU.mult))
            link(V.tensor_tensor(bw[:, 3, :], mv1[:, :, 0], s2[:, :], ALU.mult))
            V.tensor_tensor(t2[:, :], vec[:, 4 * V_B2:4 * V_B2 + 4], bw[:, 3, :], ALU.subtract).then_inc(st2_ready, 1)
            dve.wait_ge(st2_ready, 1)

            def z(c):
                for cc, f in Z_DVE:
                    if cc == c:
                        c0, cn = ZC[c]
                        V.tensor_scalar(yT[:, f, c0:c0 + cn], yT[:, f, c0:c0 + cn], s2[:, f:f + 1], t2[:, f:f + 1],
                                        ALU.mult, ALU.add).then_inc(z_dve, 1)

            def finish(i):
                n = P if i < NT - 1 else LAST
                acc = landed(dve, ("zT", i))
                V.tensor_tensor(xs[0:n, i, :], acc[0:n, :], xs[0:n, i, :], ALU.add).then_inc(o_ready, 1)

            z(0)
            z(1)
            for i in range(4):
                finish(i)
            z(2)
            for i in range(4, NT):
                finish(i)


_INS = ['x', 'src', 'dst', 'L0_gnn_norm1_g', 'L0_gnn_norm1_b', 'L0_gnn_norm2_g', 'L0_gnn_norm2_b', 'L0_gnn_W_conv',
        'L0_gnn_b_conv', 'L0_gnn_Wq', 'L0_gnn_Wk', 'L0_gnn_Wv', 'L0_gnn_Wo', 'L0_gnn_proj']


def kernel(**inputs):
    import numpy as _np
    import concourse.bacc as _bacc
    from concourse import mybir as _mybir
    from concourse.bass_utils import run_bass_kernel_spmd as _run

    nc = _bacc.Bacc("TRN2", target_bir_lowering=False, num_devices=1)
    arrays, args = {}, []
    for name in _INS:
        a = _np.ascontiguousarray(inputs[name])
        arrays[f"in_{name}"] = a
        args.append(nc.dram_tensor(f"in_{name}", a.shape, _mybir.dt.from_np(a.dtype), kind="ExternalInput").ap())
    out = nc.dram_tensor("out", (N, D), F32, kind="ExternalOutput").ap()
    gnn_kernel(nc, *args, out)
    r = _run(nc, [arrays], core_ids=[0])
    return r.results[0]["out"]
```

```python
from contextlib import ExitStack

import concourse.bass as bass
from concourse import mybir

ALU = mybir.AluOpType
ACT = mybir.ActivationFunctionType
AX_X = mybir.AxisListType.X
F32 = mybir.dt.float32
F16 = mybir.dt.float16
I32 = mybir.dt.int32
U32 = mybir.dt.uint32
ds = bass.ds

P = 128
N = 1250
D = 512
E = 20000
NT = (N + P - 1) // P
LAST = N - (NT - 1) * P
FT = D // P
HEADS, DH, M = 8, 64, 256
NA = 256
AT = NA // P
EPS, KEPS = 1e-5, 1e-6
QK_SCALE = DH ** -0.25
PHI_SCALE = 1.0 / M ** 0.5

W = 10
NW = N // W
GW = 5
NGRP = NW // GW
K = 2
CAP = K * P
GR = 16
NSTEP = NW * K
WIN0 = [0, NW // 2]
GROWS = (NW - WIN0[1]) * K
USED = [WIN0[1] * K, GROWS]
NROW = E // GR + (K - 1) * P // GR
FULL = (E - P) // GR + 1
TAIL0 = FULL * GR
TAILN = (NROW - FULL - 1) * GR + P
SLOTS = GW * K
WS = 25
NWS = N // WS
HSCALE = 2048.0
CHUNKS = [(0, 500), (500, 500), (1000, 250)]
LN_GROUPS = [(0, 2), (2, 6), (6, 10)]
ZC = [(0, 256), (256, 384), (640, 384), (1024, N - 1024)]
Z_ACT = [(0, 3)] + [(c, f) for c in (1, 2, 3) for f in (1, 2, 3)]
Z_DVE = [(0, 0), (0, 1), (0, 2), (1, 0), (2, 0), (3, 0)]
SLOW_LINKS = 8
DEG_FIRST = [FT, 0, 1, 2, 3]
EP, EJ = 125, E // 125


def gnn_kernel(nc, x, src, dst, g1, b1, g2, b2, w_conv, b_conv, w_q, w_k, w_v, w_o, proj, out):
    edges = nc.dram_tensor("edges_overlapped", [NROW, 2 * P], I32, kind="Internal").ap()

    with ExitStack() as ctx:
        def sb(name, shape, dt):
            return ctx.enter_context(nc.sbuf_tensor(name, shape, dt))

        def sem(name):
            return ctx.enter_context(nc.semaphore(name))

        bank = [ctx.enter_context(nc.psum_tensor(f"bank{i}", [P, 512], F32)) for i in range(8)]

        r1 = sb("r1", [P, FT * N], F32)
        r2 = sb("r2", [P, 5120], F32)
        r3 = sb("r3", [P, NT * N // 2], F32)
        r4 = sb("r4", [P, 2 * N], F32)
        wq = r1[:, 0:2048].rearrange("p (t n) -> p t n", t=FT)
        wk = r1[:, 2048:4096].rearrange("p (t n) -> p t n", t=FT)
        aggT = r1[:, :].rearrange("p (t n) -> p t n", t=FT)
        kf = r2[:, 0:4096].rearrange("p (t h m) -> p t h m", t=AT, h=HEADS)
        kT = r2[:, 4096:5120].rearrange("p (t n) -> p t n", t=FT)
        yT = r2[:, 0:FT * N].rearrange("p (t n) -> p t n", t=FT)
        qfT = r1[:, 0:4096].rearrange("p (t h n) -> p t h n", t=2, h=HEADS)
        A16 = r3[:, :].bitcast(F16).rearrange("p (a n) -> p a n", a=NT)
        sq = r4[:, 0:2048].rearrange("p (q t n) -> p q t n", q=2, t=FT)
        deg = r4[:, 0:N]
        rdeg = r4[:, N:2 * N]

        xs = sb("xs", [P, NT, D], F32)
        hring = sb("hring", [P, 2, D], F32)
        h1 = sb("h1", [P, NT, D], F16)
        h2 = sb("h2", [P, NT, D], F16)
        hT = sb("hT", [P, FT, N], F32)
        wc = sb("wc", [P, FT, D], F32)
        wvo = sb("wvo", [P, FT, D], F32)
        ohb = sb("ohb", [P, 2 * SLOTS, P], F16)
        ohv = sb("ohv", [P, 2 * SLOTS, NT * W], F16)
        qT = sb("qT", [P, FT, NA], F32)
        v1 = sb("v1", [P, AT, HEADS, DH + 1], F32)
        qe = sb("qe", [P, 4, AT, M], F32)
        kv = sb("kv", [P, 2, HEADS, DH + 1], F32)
        attn = qe[:, 0:2, :, :].rearrange("p q t m -> p q (t m)")
        attnT = qe[:, 2:4, :, :].rearrange("p q t m -> p (q t) m")
        haT = sb("haT", [P, FT, NA], F32)
        has_in = sb("has_in", [P, CHUNKS[0][1]], F32)

        edst = sb("edst", [EP, EJ], I32)
        esrc = sb("esrc", [EP, EJ], I32)
        tail = r2[0:1, 2848:2848 + 2 * TAILN].bitcast(I32).rearrange("p (k n) -> p k n", k=2)
        iota_i = sb("iota_i", [P, NT * WS], I32)
        iota16 = sb("iota16", [P, NT * WS], F16)
        thr_i = sb("thr_i", [P, NW], I32)
        thr = sb("thr", [P, NW], F32)
        rowc_i = sb("rowc_i", [P, 4], I32)
        rowc = sb("rowc", [P, 4], F32)
        below = r2[0:EP, 0:NW * (EJ // GR)].rearrange("p (w j) -> p w j", w=NW)
        nbelow = r2[0:EP, 1280:1280 + NW]
        nbelow4 = r2[0:EP, 1408:1408 + NSTEP].rearrange("p (w k) -> p w k", w=NW)
        edstf = r2[0:EP, 1664:1664 + EJ // GR]
        first = sb("first", [P, 2], F32)
        rows = sb("rows", [P, 2], I32)
        g = r2[0:GROWS, 0:512].bitcast(I32).rearrange("p (q e) -> p q e", q=2)
        gb_i = r2[0:GROWS, 512:768].bitcast(I32).rearrange("p (q e) -> p q e", q=2)
        ga_i = r2[0:GROWS, 768:1024].bitcast(I32).rearrange("p (q e) -> p q e", q=2)
        gb = r2[0:GROWS, 1024:1280].rearrange("p (q e) -> p q e", q=2)
        gd = r2[0:GROWS, 1280:1536].rearrange("p (q e) -> p q e", q=2)
        gx = r2[0:GROWS, 1536:1792].rearrange("p (q e) -> p q e", q=2)
        gv = r2[0:GROWS, 1792:2048].rearrange("p (q e) -> p q e", q=2)
        nout = sb("nout", [GROWS, 2], F32)
        bcol = sb("bcol", [P, NSTEP, 2], F16)
        vcol = sb("vcol", [P, NSTEP, 2], F16)
        fl = sb("fl", [1, 2], F32)
        flag = sb("flag", [1, 1], I32)

        ident = sb("ident", [P, P], F32)
        ones = sb("ones", [P, P], F32)
        c2048 = sb("c2048", [P, P], F16)
        asum = hring[:, :, :].rearrange("p q n -> p (q n)").bitcast(F16)
        half2 = sb("half2", [P, 2], F32)
        keps = sb("keps", [P, 1], F32)
        vrow = sb("vrow", [20, P], F32)
        vec = sb("vec", [P, 20], F32)
        pj = sb("pj", [P, 2, 2 * DH], F32)
        pT = sb("pT", [P, M], F32)
        st = sb("st", [P, NT, 6], F32)
        mv = sb("mv", [P, NT, 2], F32)
        lnw = sb("lnw", [P, 4, NT], F32)
        st1 = sb("st1", [P, FT, 3, 6], F32)
        mv1 = sb("mv1", [P, FT, 2], F32)
        bw = sb("bw", [P, 6, FT], F32)
        s1 = sb("s1", [P, FT], F32)
        t1 = sb("t1", [P, FT], F32)
        s2 = sb("s2", [P, FT], F32)
        t2 = sb("t2", [P, FT], F32)
        mxk = sb("mxk", [P, AT, HEADS], F32)
        mxk1 = sb("mxk1", [P, HEADS], F32)
        mk8 = sb("mk8", [HEADS, 1], F32)
        dg8 = sb("dg8", [HEADS, HEADS], F32)
        mxq = sb("mxq", [P, AT, HEADS], F32)
        diag = sb("diag", [P, 2, AT, HEADS], F32)
        kb = sb("kb", [P, AT, HEADS], F32)
        qb = sb("qb", [P, AT, HEADS], F32)
        zz = sb("zz", [P, 4, 4], F32)
        zr = sb("zr", [P, 4, 4], F32)

        si = r2[0:EP, 0:2 * EJ].bitcast(I32).rearrange("p (k j) -> p k j", k=2)
        sa = r2[0:EP, 2 * EJ:3 * EJ]
        sbb = r2[0:EP, 3 * EJ:4 * EJ]
        sd = r2[0:EP, 4 * EJ:5 * EJ]
        sx = r2[0:EP, 5 * EJ:6 * EJ]
        sv = r2[0:EP, 6 * EJ:7 * EJ]
        sw = r2[0:EP, 7 * EJ:8 * EJ]
        sohb = r2[0:EP, 1280:1792].bitcast(F16).rearrange("p (s n) -> p s n", s=8)
        sohv = r2[0:EP, 1792:1792 + 4 * NT * WS].bitcast(F16).rearrange("p (s n) -> p s n", s=8)
        wbase = sb("wbase", [EP, 1], F32)
        aw = sb("aw", [P, 2, NT, WS], F16)
        zero16 = sb("zero16", [P, NT * WS], F16)

        V_G1, V_B1, V_G2, V_B2, V_BC = range(5)

        order = [("first", 6)]
        for i in range(NT):
            order += [(("hT", i), 4 + i % 2)]
            order += {1: [(("q", 0), 2)], 3: [(("q", 1), 3), ("cols", 7), ("out", 6)],
                      5: [("vec", 7), ("proj", 6), (("k", 0), 2), ("diag", 7)], 7: [(("k", 1), 3)]}.get(i, [])
        order += [(("v", i), 4 + i) for i in range(2)]
        order += [(("uk", i), 3 + i % 4) for i in range(8)]
        order += [("kmaxT", 7), ("kmax", 7)]
        order += [(("uq", i), 3 + i % 4) for i in range(8)]
        order += [(("qfT", h), 2 if h % 2 else 7) for h in range(HEADS)]
        order += [(("agg", 0, FT), 3), (("agg", 0, 0), 4)]
        order += [(("kv", i), (5, 6, 2, 7)[i]) for i in range(4)]
        order += [(("attn", i), (5, 6, 2, 7)[i]) for i in range(4)]
        order += [(("agg", 0, 1), 5), (("agg", 0, 2), 6)]
        order += [(("attnT", i), (2, 7)[i]) for i in range(2)]
        order += [(("ha", i), 3 + i) for i in range(2)]
        agg_banks = iter([2, 7, 5, 6, 3, 4, 2, 7, 5, 0, 1])
        order += [(("agg", c, f), next(agg_banks)) for c in range(3) for f in DEG_FIRST if c or f == 3]
        cycle = [3, 4, 6, 2, 7, 5, 0, 1]
        order_after = [(("conv", c, f), cycle[(c * FT + f) % 8]) for c in range(3) for f in range(FT)]
        order_after += [(("zT", i), cycle[(3 * FT + i) % 8]) for i in range(NT)]
        uses = {}
        nuse = [0] * 8
        for name, b in order + order_after:
            nuse[b] += 1
            uses[name] = (b, nuse[b])
        bank_full = [sem(f"bank_full{b}") for b in range(8)]
        bank_read = [sem(f"bank_read{b}") for b in range(8)]

        def pe_open(pe, name):
            b, n = uses[name]
            if n > 1:
                pe.wait_ge(bank_read[b], n - 1)
            return bank[b]

        def full(name):
            return bank_full[uses[name][0]]

        def read(name):
            return bank_read[uses[name][0]]

        def stored(eng, name):
            b, n = uses[name]
            eng.wait_ge(bank_read[b], n)

        def landed(eng, name):
            b, n = uses[name]
            eng.wait_ge(bank_full[b], n)
            return bank[b]

        x_in = [sem(f"x_in{i}") for i in range(NT)]
        pad_zero = sem("pad_zero")
        dst_in = sem("dst_in")
        src_in = sem("src_in")
        tail_set = sem("tail_set")
        tail_in = sem("tail_in")
        ov_out = sem("ov_out")
        vec_in = sem("vec_in")
        pj_in = sem("pj_in")
        wq_in = sem("wq_in")
        wk_in = sem("wk_in")
        wv_in = sem("wv_in")
        wo_in = sem("wo_in")
        wc_in = sem("wc_in")
        id_set = sem("id_set")
        cst_set = sem("cst_set")
        dve_cst = sem("dve_cst")
        iota_set = sem("iota_set")
        ln_var = sem("ln_var")
        ln_std = sem("ln_std")
        ln_ready = sem("ln_ready")
        h_ready = sem("h_ready")
        h1_ready = sem("h1_ready")
        h_split = sem("h_split")
        rows_ready = sem("rows_ready")
        g_in = [sem(f"g_in{i}") for i in range(2)]
        g_ready = sem("g_ready")
        nb_ready = sem("nb_ready")
        cols_ready = sem("cols_ready")
        flag_ready = sem("flag_ready")
        vec_ready = sem("vec_ready")
        pT_ready = sem("pT_ready")
        hT_ready = sem("hT_ready")
        qk_ready = sem("qk_ready")
        sq_ready = sem("sq_ready")
        v_ready = sem("v_ready")
        uk_copied = sem("uk_copied")
        kmax_part = sem("kmax_part")
        kmax_diag = sem("kmax_diag")
        k_exp = sem("k_exp")
        kf_ready = sem("kf_ready")
        qb_ready = sem("qb_ready")
        q_exp = sem("q_exp")
        qe_used = sem("qe_used")
        qfT_ready = sem("qfT_ready")
        kv_ready = sem("kv_ready")
        attn_ready = sem("attn_ready")
        attnT_ready = sem("attnT_ready")
        haT_ready = sem("haT_ready")
        hTa_ready = sem("hTa_ready")
        bn_var = sem("bn_var")
        bn_std = sem("bn_std")
        oh_ready = sem("oh_ready")
        group_counted = sem("group_counted")
        group_stored = sem("group_stored")
        sums_final = sem("sums_final")
        mean_ready = sem("mean_ready")
        asum_ready = sem("asum_ready")
        y_ready = sem("y_ready")
        st2_ready = sem("st2_ready")
        z_act = sem("z_act")
        z_dve = sem("z_dve")
        o_ready = sem("o_ready")
        o_out = sem("o_out")
        s_oh = sem("s_oh")
        s_used = sem("s_used")
        s_link = sem("s_link")
        s_prep = sem("s_prep")
        s_count = sem("s_count")
        s_aw = sem("s_aw")
        s_agg = sem("s_agg")
        s_read = sem("s_read")
        dve_step = sem("dve_step")
        act_step = sem("act_step")
        pool_step = sem("pool_step")

        block = ctx.enter_context(nc.Block())

        @block.sync
        def _(sp):
            sp.dma_start(edst[:, :], dst.rearrange("(p j) -> p j", p=EP)).then_inc(dst_in, 16)
            for i in range(NT):
                n = P if i < NT - 1 else LAST
                if i == NT - 1:
                    sp.wait_ge(pad_zero, 1)
                sp.dma_start(xs[0:n, i, :], x[i * P:i * P + n, :]).then_inc(x_in[i], 16)
                if i == 3:
                    sp.dma_start(wq, w_q.rearrange("(t p) n -> p t n", p=P)).then_inc(wq_in, 16)
                    sp.wait_ge(tail_in, 32)
                    t_ap = tail[:, :, :]
                    for k in range(2):
                        sp.dma_start(edges[FULL:NROW, k * P:(k + 1) * P].rearrange("(o r) e -> o r e", o=1),
                                     bass.AP(t_ap.tensor, t_ap.offset + k * TAILN,
                                             [list(t_ap.ap[0]), [GR, NROW - FULL], [1, P]])).then_inc(ov_out, 16)
            for k, v in enumerate((g1, b1, g2, b2, b_conv)):
                sp.dma_start(vrow[4 * k:4 * k + 4, :], v.rearrange("(t p) -> t p", p=P)).then_inc(vec_in, 16)
            for k in range(2):
                sp.dma_start(pj[:, :, k * DH:(k + 1) * DH], proj.rearrange("(t p) d -> p t d", p=P)).then_inc(pj_in, 16)
            sp.dma_start(wk, w_k.rearrange("(t p) n -> p t n", p=P)).then_inc(wk_in, 16)
            sp.dma_start(wvo[:, :, :], w_v.rearrange("(t p) n -> p t n", p=P)).then_inc(wv_in, 16)
            sp.dma_start(wc[:, :, :], w_conv.rearrange("(t p) n -> p t n", p=P)).then_inc(wc_in, 16)
            for t in range(AT):
                landed(sp, ("v", t))
            sp.dma_start(wvo[:, :, :], w_o.rearrange("(t p) n -> p t n", p=P)).then_inc(wo_in, 16)
            sp.dma_start(esrc[:, :], src.rearrange("(p j) -> p j", p=EP)).then_inc(src_in, 16)
            for i in range(NT):
                n = P if i < NT - 1 else LAST
                sp.wait_ge(o_ready, i + 1)
                sp.dma_start(out[i * P:i * P + n, :], xs[0:n, i, :]).then_inc(o_out, 16)
            sp.wait_ge(src_in, 16)
            sp.wait_ge(o_out, 16 * NT)

        @block.gpsimd
        def _(pool):
            pool.memset(tail[:, :, :], -1).then_inc(tail_set, 1)
            pool.memset(xs[:, NT - 1, :], 0.0).then_inc(pad_zero, 1)
            pool.iota(thr_i[:, :], [[W, NW]], base=0, channel_multiplier=0).then_inc(iota_set, 1)
            pool.iota(rowc_i[:, 0:1], [[0, 1]], base=0, channel_multiplier=1).then_inc(iota_set, 1)
            pool.iota(iota_i[:, :], [[1, NT * WS]], base=0, channel_multiplier=0).then_inc(iota_set, 1)
            pool.memset(ident[:, :], 0.0).then_inc(pool_step, 1)
            pool.wait_ge(pool_step, 1)
            pool.affine_select(out=ident[:, :], in_=ident[:, :], compare_op=ALU.not_equal, fill=1.0, base=0,
                               pattern=[[-1, P]], channel_multiplier=1).then_inc(id_set, 1)
            pool.memset(v1[:, :, :, DH:DH + 1], 1.0).then_inc(cst_set, 1)
            pool.memset(keps[:, :], KEPS).then_inc(cst_set, 1)
            pool.memset(c2048[:, :], HSCALE).then_inc(cst_set, 1)
            pool.memset(zero16[:, :], 0.0).then_inc(cst_set, 1)
            pool.memset(half2[:, :], 0.0).then_inc(pool_step, 1)
            pool.wait_ge(pool_step, 2)
            pool.memset(half2[0:DH, 0:1], 0.5).then_inc(cst_set, 1)
            pool.memset(half2[DH:P, 1:2], 0.5).then_inc(cst_set, 1)
            pool.wait_ge(ov_out, 16 * 4)
            pool.wait_ge(rows_ready, 1)
            for hf in range(2):
                pool.indirect_dma_start(out=g[:, hf, :], out_offset=None, in_=edges,
                                        in_offset=bass.IndirectOffsetOnAxis(ap=rows[0:GROWS, hf:hf + 1], axis=0),
                                        ).then_inc(g_in[hf], 16)

        @block.scalar
        def _(act):
            for k, e in enumerate((src, dst)):
                act.dma_start(edges[0:FULL, k * P:(k + 1) * P],
                              bass.AP(e.tensor, 0, [[GR, FULL], [1, P]])).then_inc(ov_out, 16)
            act.wait_ge(tail_set, 1)
            for k, e in enumerate((src, dst)):
                act.dma_start(tail[:, k, 0:E - TAIL0], e[TAIL0:E].rearrange("(o n) -> o n", o=1)).then_inc(tail_in, 16)
            def store_hT(i):
                n = P if i < NT - 1 else LAST
                acc = landed(act, ("hT", i))
                act.activation(hT[:, :, i * P:i * P + n], acc[:, :].rearrange("p (t n) -> p t n", t=FT)[:, :, 0:n],
                               ACT.Copy).then_inc(read(("hT", i)), 1)

            stores = [0]

            def store():
                p = stores[0]
                stores[0] += 1
                act.wait_ge(group_counted, p + 1)
                act.activation(A16[:, :, p * GW * W:(p + 1) * GW * W].rearrange("p a (q d) -> p q a d", q=GW),
                               bank[p % 2][:, 0:GW * NT * W].rearrange("p (q a d) -> p q a d", q=GW, a=NT),
                               ACT.Copy).then_inc(group_stored, 1)

            def ln_tile(i):
                if i >= 2:
                    act.wait_ge(h_split, i - 1)
                    act.wait_ge(full(("hT", i - 2)), uses[("hT", i - 2)][1])
                act.activation(hring[:, i % 2, :], xs[:, i, :], ACT.Relu,
                               bias=lnw[:, 3, i:i + 1], scale=lnw[:, 2, i:i + 1]).then_inc(h_ready, 1)
                if i not in (0, 2):
                    store_hT(i - 1)
                act.wait_ge(h_ready, i + 1)
                act.activation(h1[:, i, :], hring[:, i % 2, :], ACT.Copy, scale=HSCALE).then_inc(h1_ready, 1)

            def qk(j, i):
                nm, tT = (("q", qT), ("k", kT))[j]
                acc = landed(act, (nm, i))
                act.activation(tT[:, 2 * i:2 * i + 2, :], acc[:, :].rearrange("p (t n) -> p t n", t=2),
                               ACT.Copy, scale=QK_SCALE).then_inc(read((nm, i)), 1)
                stored(act, (nm, i))
                act.activation(sq[:, j, 2 * i:2 * i + 2, :], tT[:, 2 * i:2 * i + 2, :], ACT.Square).then_inc(sq_ready, 1)

            def ln_std_of(gi):
                a, b = LN_GROUPS[gi]
                act.wait_ge(ln_var, gi + 1)
                act.activation(lnw[:, 1, a:b], lnw[:, 0, a:b], ACT.Sqrt).then_inc(ln_std, 1)

            ln_std_of(0)
            act.wait_ge(ln_ready, 1)
            ln_tile(0)
            ln_tile(1)
            store_hT(1)
            ln_std_of(1)
            act.wait_ge(ln_ready, 2)
            ln_tile(2)
            ln_tile(3)
            ln_std_of(2)
            qk(0, 0)
            ln_tile(4)
            ln_tile(5)
            qk(0, 1)
            act.wait_ge(ln_ready, 3)
            ln_tile(6)
            ln_tile(7)
            qk(1, 0)
            store()
            ln_tile(8)
            ln_tile(9)
            store_hT(NT - 1)
            qk(1, 1)

            def store_v(t):
                acc = landed(act, ("v", t))
                act.wait_ge(cst_set, 6)
                act.activation(v1[:, t, :, 0:DH], acc[:, :].rearrange("p (h d) -> p h d", h=HEADS), ACT.Copy
                               ).then_inc(read(("v", t)), 1)

            store()
            store_v(0)
            act.wait_ge(bn_var, 1)
            act.activation(bw[:, 1, :], bw[:, 0, :], ACT.Sqrt).then_inc(bn_std, 1)
            store()
            store_v(1)
            store()
            act.wait_ge(bank_full[uses["cols"][0]], uses["cols"][1])
            for h in range(HEADS):
                acc = landed(act, ("uk", h))
                act.activation(kf[:, :, h, :], acc[:, :].rearrange("p (t m) -> p t m", t=AT),
                               ACT.Copy).then_inc(read(("uk", h)), 1)
                if h == 2:
                    store()

            def q_feat(h):
                acc = landed(act, ("qfT", h))
                if h == 1:
                    landed(act, ("k", 1))
                    act.wait_ge(cst_set, 6)
                act.activation(qfT[:, :, h, :], acc[:, :].rearrange("p (m n) -> p m n", m=2), ACT.Identity,
                               bias=keps[:, 0:1], scale=PHI_SCALE).then_inc(read(("qfT", h)), 1)

            def k_exps(t, half):
                for h in range(4 * half, 4 * half + 4):
                    act.activation(kf[:, t, h, :], kf[:, t, h, :], ACT.Exp, bias=kb[:, t, h:h + 1]).then_inc(k_exp, 1)

            for h in range(HEADS):
                acc = landed(act, ("uq", h))
                act.wait_ge(qb_ready, h + 1)
                if h >= 4:
                    act.wait_ge(full(("qfT", h - 4)), uses[("qfT", h - 4)][1])
                act.activation(qe[:, h % 4, 0, :], acc[:, 0:M], ACT.Exp, bias=qb[:, 0, h:h + 1])
                act.activation(qe[:, h % 4, 1, :], acc[:, M:2 * M], ACT.Exp, bias=qb[:, 1, h:h + 1]).then_inc(read(("uq", h)), 1)
                if h == 4 or h == 6:
                    q_feat(h - 3)
                if h % 2:
                    store()
                if h == 1:
                    stored(act, "kmax")
                if h in (1, 2, 4, 6):
                    k_exps(*divmod((1, 2, 4, 6).index(h), 2))
            q_feat(5)
            store()
            q_feat(7)

            while stores[0] < NGRP:
                store()

            for c, (c0, cn) in enumerate(CHUNKS):
                for f in range(FT):
                    acc = landed(act, ("conv", c, f))
                    act.activation(yT[:, f, c0:c0 + cn], acc[:, 0:cn], ACT.Relu,
                                   bias=vec[:, 4 * V_BC + f:4 * V_BC + f + 1]).then_inc(read(("conv", c, f)), 1)
            act.wait_ge(bn_var, 2)
            act.activation(bw[:, 1, :], bw[:, 0, :], ACT.Sqrt).then_inc(bn_std, 1)
            act.wait_ge(st2_ready, 1)
            for c, f in Z_ACT:
                c0, cn = ZC[c]
                act.activation(yT[:, f, c0:c0 + cn], yT[:, f, c0:c0 + cn], ACT.Identity,
                               bias=t2[:, f:f + 1], scale=s2[:, f:f + 1]).then_inc(z_act, 1)

        @block.tensor
        def _(pe):
            pe.wait_ge(id_set, 1)
            pe.wait_ge(dve_cst, 1)
            pe.wait_ge(nb_ready, 1)
            acc = pe_open(pe, "first")
            for hf in range(2):
                last = nc.tensor.matmul(acc[0:GROWS, hf:hf + 1],
                                        nbelow4[:, WIN0[hf]:WIN0[hf] + GROWS // K, :].rearrange("p w k -> p (w k)"),
                                        ones[0:EP, 0:1], start=True, stop=True)
            last.then_inc(full("first"), 1)
            def transpose_h(i):
                pe.wait_ge(h_ready, i + 1)
                acc = pe_open(pe, ("hT", i))
                for f in range(FT):
                    last = nc.tensor.transpose(acc[:, f * P:(f + 1) * P], hring[:, i % 2, f * P:(f + 1) * P], ident[:, :])
                last.then_inc(full(("hT", i)), 1)

            def qk(nm, w, i):
                acc = pe_open(pe, (nm, i))
                for t in range(2):
                    c = (2 * i + t) * P
                    for f in range(FT):
                        last = nc.tensor.matmul(acc[:, t * NA:(t + 1) * NA], w[:, f, c:c + P], hT[:, f, 0:NA],
                                                start=(f == 0), stop=(f == FT - 1))
                last.then_inc(full((nm, i)), 1)

            counts = [0]

            def count():
                p = counts[0]
                counts[0] += 1
                pe.wait_ge(oh_ready, p + 1)
                if p >= 2:
                    pe.wait_ge(group_stored, p - 1)
                for q in range(GW):
                    for k in range(K):
                        s = p % 2 * SLOTS + q * K + k
                        last = nc.tensor.matmul(bank[p % 2][:, q * NT * W:(q + 1) * NT * W], ohb[:, s, :], ohv[:, s, :],
                                                start=(k == 0), stop=(k == K - 1))
                last.then_inc(group_counted, 1)

            def diagonal(j, t):
                pe.wait_ge(sq_ready, 2 * (j + 1))
                if (j, t) == (0, 0):
                    pe.wait_ge(cst_set, 6)
                    pe_open(pe, "diag")
                acc = bank[uses["diag"][0]]
                for c in range(FT):
                    o = (j * AT + t) * HEADS + 2 * c
                    last = nc.tensor.matmul(acc[:, o:o + 2], sq[:, j, c, t * P:(t + 1) * P], half2[:, :],
                                            start=True, stop=True)
                if (j, t) == (1, 1):
                    last.then_inc(full("diag"), 1)

            transpose_h(0)
            transpose_h(1)
            for i in range(2):
                stored(pe, ("hT", i))
            pe.wait_ge(wq_in, 16)
            qk("q", wq, 0)
            transpose_h(2)
            transpose_h(3)
            qk("q", wq, 1)
            pe.wait_ge(g_ready, 1)
            acc = pe_open(pe, "cols")
            for j, m in enumerate((gb, gv)):
                for hf in range(2):
                    o, n = j * NSTEP + hf * USED[0], USED[hf]
                    last = nc.tensor.transpose(acc[:, o:o + n], m[0:n, hf, :], ident[0:n, 0:n])
            last.then_inc(full("cols"), 1)
            acc = pe_open(pe, "out")
            for hf in range(2):
                last = nc.tensor.matmul(acc[0:1, 0:1], nout[0:USED[hf], hf:hf + 1], ones[0:USED[hf], 0:1],
                                        start=(hf == 0), stop=(hf == 1))
            last.then_inc(full("out"), 1)
            transpose_h(4)
            transpose_h(5)
            pe.wait_ge(vec_in, 16 * 5)
            acc = pe_open(pe, "vec")
            nc.tensor.transpose(acc[:, 0:20], vrow[:, :], ident[0:20, 0:20]).then_inc(full("vec"), 1)
            pe.wait_ge(pj_in, 32)
            acc = pe_open(pe, "proj")
            for t in range(2):
                last = nc.tensor.transpose(acc[:, t * P:(t + 1) * P], pj[:, t, :], ident[:, :])
            last.then_inc(full("proj"), 1)
            pe.wait_ge(wk_in, 16)
            qk("k", wk, 0)
            diagonal(0, 0)
            count()
            for i in range(6, NT):
                transpose_h(i)
                if i == 7:
                    qk("k", wk, 1)
                    diagonal(0, 1)
                    count()

            def aggregate(c, f):
                c0, cn = CHUNKS[c]
                pe.wait_ge(group_stored, -(-(c0 + cn) // (GW * W)))
                pe.wait_ge(h_split, NT)
                acc = pe_open(pe, ("agg", c, f))
                if f == FT and c > 0:
                    pe.wait_ge(asum_ready, c)
                    nc.tensor.matmul(acc[:, 0:cn], c2048[:, :], asum[:, 0:cn], start=True, stop=True
                                     ).then_inc(full(("agg", c, f)), 1)
                    return
                for s in range(NT):
                    for hh in (h1, h2) if f < FT else (c2048,):
                        lhs = hh[:, s, f * P:(f + 1) * P] if f < FT else c2048[:, :]
                        last = nc.tensor.matmul(acc[:, 0:cn], lhs, A16[:, s, c0:c0 + cn],
                                                start=(s == 0 and hh is not h2), stop=(s == NT - 1 and hh is not h1))
                last.then_inc(full(("agg", c, f)), 1)

            pe.wait_ge(wv_in, 16)
            for t in range(AT):
                acc = pe_open(pe, ("v", t))
                for f in range(FT):
                    last = nc.tensor.matmul(acc[:, :], hT[:, f, t * P:(t + 1) * P], wvo[:, f, :],
                                            start=(f == 0), stop=(f == FT - 1))
                last.then_inc(full(("v", t)), 1)
                diagonal(1, t)
                count()
            def features(nm, tT, h):
                p0 = h % 2 * DH
                acc = pe_open(pe, (nm, h))
                for t in range(AT):
                    last = nc.tensor.matmul(acc[:, t * M:(t + 1) * M], tT[p0:p0 + DH, h // 2, t * P:(t + 1) * P],
                                            pT[p0:p0 + DH, :], start=True, stop=True)
                last.then_inc(full((nm, h)), 1)

            def transpose_qf(h):
                acc = pe_open(pe, ("qfT", h))
                stored(pe, ("uq", h))
                for m in range(2):
                    for t in range(2):
                        o = (2 * m + t) * P
                        last = nc.tensor.transpose(acc[:, o:o + P], qe[:, h % 4, t, m * P:(m + 1) * P], ident[:, :])
                last.then_inc(full(("qfT", h)), 1)

            stored(pe, "proj")
            for i in range(8):
                features("uk", kT, i)
                if i == 1:
                    count()
            features("uq", qT, 0)
            features("uq", qT, 1)
            count()
            pe.wait_ge(kmax_part, 1)
            acc = pe_open(pe, "kmaxT")
            nc.tensor.transpose(acc[0:HEADS, 0:P], mxk1[:, :], ident[:, :]).then_inc(full("kmaxT"), 1)
            features("uq", qT, 2)
            pe.wait_ge(kmax_diag, 1)
            acc = pe_open(pe, "kmax")
            nc.tensor.matmul(acc[:, 0:HEADS], ones[0:HEADS, :], dg8[:, :], start=True, stop=True).then_inc(full("kmax"), 1)
            features("uq", qT, 3)
            count()
            for hp in range(4):
                transpose_qf(2 * hp)
                transpose_qf(2 * hp + 1)
                if hp < 2:
                    features("uq", qT, 2 * hp + 4)
                    features("uq", qT, 2 * hp + 5)
                if hp < 3:
                    count()
            aggregate(0, FT)

            aggregate(0, 0)
            for i in range(4):
                m, half = divmod(i, 2)
                acc = pe_open(pe, ("kv", i))
                pe.wait_ge(kf_ready, 2)
                stored(pe, ("v", 0))
                stored(pe, ("v", 1))
                for j in range(4):
                    h = 4 * half + j
                    for t in range(AT):
                        last = nc.tensor.matmul(acc[:, j * (DH + 1):(j + 1) * (DH + 1)], kf[:, t, h, m * P:(m + 1) * P],
                                                v1[:, t, h, :], start=(t == 0), stop=(t == AT - 1))
                last.then_inc(full(("kv", i)), 1)
                count()
            for h in range(HEADS):
                stored(pe, ("qfT", h))
            for i in range(4):
                stored(pe, ("kv", i))
            for i in range(4):
                t, half = divmod(i, 2)
                acc = pe_open(pe, ("attn", i))
                for j in range(4):
                    h = 4 * half + j
                    for m in range(2):
                        last = nc.tensor.matmul(acc[:, j * (DH + 1):(j + 1) * (DH + 1)], qfT[:, m, h, t * P:(t + 1) * P],
                                                kv[:, m, h, :], start=(m == 0), stop=(m == 1))
                last.then_inc(full(("attn", i)), 1)
                if i % 2:
                    count()
            aggregate(0, 1)
            count()
            for i in range(4):
                stored(pe, ("attn", i))
            for i in range(2):
                acc = pe_open(pe, ("attnT", i))
                for c in range(2):
                    for t in range(AT):
                        o = (2 * c + t) * P
                        last = nc.tensor.transpose(acc[:, o:o + P], attn[:, t, (2 * i + c) * P:(2 * i + c + 1) * P], ident[:, :])
                last.then_inc(full(("attnT", i)), 1)
            count()
            aggregate(0, 2)
            count()
            pe.wait_ge(wo_in, 16)
            for i in range(2):
                stored(pe, ("attnT", i))
            for i in range(2):
                acc = pe_open(pe, ("ha", i))
                for t in range(2):
                    o = (2 * i + t) * P
                    for c in range(FT):
                        last = nc.tensor.matmul(acc[:, t * NA:(t + 1) * NA], wvo[:, c, o:o + P], attnT[:, c, :],
                                                start=(c == 0), stop=(c == FT - 1))
                last.then_inc(full(("ha", i)), 1)
                if i == 0:
                    count()

            aggregate(0, 3)
            count()
            for f in DEG_FIRST:
                aggregate(1, f)
                if f != 3:
                    count()
            for f in DEG_FIRST:
                aggregate(2, f)

            pe.wait_ge(flag_ready, 1)
            covered = pe.value_load(flag[0:1, 0:1], min_val=0, max_val=1)
            with pe.If(covered == 0):
                for c in range(3):
                    for f in DEG_FIRST:
                        stored(pe, ("agg", c, f))
                with pe.Fori(0, NWS) as w:
                    nc.tensor.matmul(bank[0][:, 0:NT * WS], zero16[:, 0:P], zero16[:, :], start=True, stop=False)
                    with pe.Fori(0, EJ // 8) as gg:
                        pe.wait_ge(s_oh, w * (EJ // 8) + gg + 1)
                        for s in range(8):
                            last = nc.tensor.matmul(bank[0][:, 0:NT * WS], sohb[:, s, :], sohv[:, s, :],
                                                    start=False, stop=False)
                        last.then_inc(s_used, 1)
                    nc.tensor.matmul(bank[0][:, 0:NT * WS], zero16[:, 0:P], zero16[:, :], start=False, stop=True).then_inc(s_count, 1)
                    pe.wait_ge(s_aw, w + 1)
                    for f in range(FT + 1):
                        for s in range(NT):
                            for hl in range(2):
                                for hh in (h1, h2) if f < FT else (c2048,):
                                    lhs = hh[:, s, f * P:(f + 1) * P] if f < FT else c2048[:, :]
                                    last = nc.tensor.matmul(bank[2 + f][:, 0:WS], lhs, aw[:, hl, s, :],
                                                            start=(s == 0 and hl == 0 and hh is not h2),
                                                            stop=(s == NT - 1 and hl == 1 and hh is not h1))
                    last.then_inc(s_agg, 1)
                    pe.wait_ge(s_read, w + 1)

            pe.wait_ge(wc_in, 16)
            pe.wait_ge(sums_final, 1)
            for c, (c0, cn) in enumerate(CHUNKS):
                pe.wait_ge(mean_ready, FT * (c + 1))
                for o in range(FT):
                    acc = pe_open(pe, ("conv", c, o))
                    for f in range(FT):
                        last = nc.tensor.matmul(acc[:, 0:cn], wc[:, f, o * P:(o + 1) * P], aggT[:, f, c0:c0 + cn],
                                         start=(f == 0), stop=(f == FT - 1))
                    last.then_inc(full(("conv", c, o)), 1)
            for i in range(NT):
                n = P if i < NT - 1 else LAST
                c = max(c for c, (c0, _) in enumerate(ZC) if c0 <= i * P)
                pe.wait_ge(z_dve, sum(1 for cc, _ in Z_DVE if cc <= c))
                pe.wait_ge(z_act, sum(1 for cc, _ in Z_ACT if cc <= c))
                if i < 8:
                    acc = pe_open(pe, ("zT", i))
                else:
                    pe.wait_ge(o_ready, i - 7)
                    acc = bank[uses[("zT", i)][0]]
                for f in range(FT):
                    last = nc.tensor.transpose(acc[0:n, f * P:(f + 1) * P], yT[:, f, i * P:i * P + n], ident[:, :])
                last.then_inc(full(("zT", i)), 1)

        @block.vector
        def _(dve):
            V = nc.vector
            step = [0]

            def link(ins):
                step[0] += 1
                ins.then_inc(dve_step, 1)
                dve.wait_ge(dve_step, step[0])

            def rstd(var, std, r, t):
                link(V.reciprocal(r, std))
                link(V.tensor_tensor(t, r, r, ALU.mult))
                link(V.tensor_tensor(t, t, var, ALU.mult))
                link(V.tensor_scalar(t, t, -0.5, 1.5, ALU.mult, ALU.add))
                link(V.tensor_tensor(r, r, t, ALU.mult))

            V.memset(ones[:, :], 1.0).then_inc(dve_cst, 1)
            dve.wait_ge(iota_set, 3)
            link(V.tensor_copy(thr[:, :], thr_i[:, :]))
            link(V.tensor_copy(iota16[:, :], iota_i[:, :]))
            link(V.tensor_scalar(rowc_i[:, 1:2], rowc_i[:, 0:1], K - 1, None, ALU.bitwise_and))
            link(V.tensor_scalar(rowc_i[:, 2:3], rowc_i[:, 0:1], K.bit_length() - 1, None, ALU.arith_shift_right))
            link(V.tensor_scalar(rowc[:, 0:1], rowc_i[:, 1:2], float(P // GR), None, ALU.mult))
            link(V.tensor_scalar(rowc[:, 1:2], rowc_i[:, 2:3], float(W), None, ALU.mult))
            link(V.tensor_scalar(rowc[:, 2:3], rowc[:, 1:2], float(W * WIN0[1]), None, ALU.add))
            dve.wait_ge(dst_in, 16)
            link(V.tensor_copy(edstf[:, :], edst[:, ::GR]))
            nj = EJ // GR
            link(V.tensor_tensor(below[:, :, :], edstf[:, :].unsqueeze(1).to_broadcast([EP, NW, nj]),
                                 thr[0:EP, :].unsqueeze(2).to_broadcast([EP, NW, nj]), ALU.is_lt))
            link(V.tensor_reduce(nbelow[:, :], below[:, :, :], AX_X, ALU.add))
            V.tensor_copy(nbelow4[:, :, :], nbelow[:, :].unsqueeze(2).to_broadcast([EP, NW, K])).then_inc(nb_ready, 1)

            def ln_stats(gi):
                a, b = LN_GROUPS[gi]
                for i in range(a, b):
                    if i == NT - 1:
                        dve.wait_ge(pad_zero, 1)
                    dve.wait_ge(x_in[i], 16)
                    ins = V.bn_stats(st[:, i, :], xs[:, i, :])
                link(ins)
                for i in range(a, b):
                    ins = V.bn_aggr(mv[:, i, :], st[:, i, :])
                link(ins)
                V.tensor_scalar(lnw[:, 0, a:b], mv[:, a:b, 1], EPS, None, ALU.add).then_inc(ln_var, 1)

            def ln_scale(gi):
                a, b = LN_GROUPS[gi]
                dve.wait_ge(ln_std, gi + 1)
                rstd(lnw[:, 0, a:b], lnw[:, 1, a:b], lnw[:, 2, a:b], lnw[:, 3, a:b])
                V.scalar_tensor_tensor(out=lnw[:, 3, a:b], in0=mv[:, a:b, 0], scalar=-1.0, in1=lnw[:, 2, a:b],
                                       op0=ALU.mult, op1=ALU.mult).then_inc(ln_ready, 1)

            def split(i):
                dve.wait_ge(h1_ready, i + 1)
                V.scalar_tensor_tensor(out=h2[:, i, :], in0=hring[:, i % 2, :], scalar=HSCALE, in1=h1[:, i, :],
                                       op0=ALU.mult, op1=ALU.subtract).then_inc(h_split, 1)

            def bn_piece(c):
                for i in range(4 * c, min(4 * c + 4, NT)):
                    stored(dve, ("hT", i))
                for f in range(FT):
                    ins = V.bn_stats(st1[:, f, c, :], hT[:, f, c * 512:min((c + 1) * 512, N)])
                if c == 2:
                    link(ins)

            groups = [0]

            def one_hots():
                p = groups[0]
                groups[0] += 1
                if p >= 2:
                    dve.wait_ge(group_counted, p - 1)
                n = SLOTS
                s0 = p % 2 * n
                for oh, col, size in ((ohb, bcol, P), (ohv, vcol, NT * W)):
                    shape = [P, n, size // 2, 2]
                    last = V.tensor_tensor(oh[:, s0:s0 + n, :].rearrange("p s (m t) -> p s m t", t=2),
                                           iota16[:, 0:size].rearrange("p (m t) -> p m t", t=2).unsqueeze(1).to_broadcast(shape),
                                           col[:, p * n:(p + 1) * n, :].unsqueeze(2).to_broadcast(shape), ALU.is_equal)
                last.then_inc(oh_ready, 1)

            dve.wait_ge(full("first"), uses["first"][1])
            V.tensor_scalar(first[0:GROWS, :], bank[uses["first"][0]][0:GROWS, 0:2], -1.0, 0.0, ALU.add, ALU.max
                            ).then_inc(read("first"), 1)
            stored(dve, "first")
            V.tensor_scalar(rows[0:GROWS, :], first[0:GROWS, :], rowc[0:GROWS, 0:1], None, ALU.add).then_inc(rows_ready, 1)
            ln_stats(0)
            ln_scale(0)
            ln_stats(1)
            split(0)
            split(1)
            ln_scale(1)
            ln_stats(2)
            split(2)
            for hf in range(2):
                dve.wait_ge(g_in[hf], 16)
            link(V.tensor_scalar(gb_i[:, :, :], g[:, :, 0:P], P - 1, None, ALU.bitwise_and))
            link(V.tensor_scalar(ga_i[:, :, :], g[:, :, 0:P], 7, None, ALU.arith_shift_right))
            for hf in range(2):
                link(V.tensor_scalar(gd[:, hf, :], g[:, hf, P:2 * P], rowc[0:GROWS, 1 + hf:2 + hf], None, ALU.subtract))
            link(V.tensor_copy(gb[:, :, :], gb_i[:, :, :]))
            link(V.tensor_scalar(gx[:, :, :], gd[:, :, :], 0.0, None, ALU.is_lt))
            link(V.scalar_tensor_tensor(out=gx[:, :, :], in0=gd[:, :, :], scalar=W - 0.5, in1=gx[:, :, :],
                                        op0=ALU.is_gt, op1=ALU.add))
            link(V.scalar_tensor_tensor(out=gv[:, :, :], in0=ga_i[:, :, :], scalar=float(W), in1=gd[:, :, :],
                                        op0=ALU.mult, op1=ALU.add))
            for hf in range(2):
                ins = V.tensor_scalar(gx[:, hf, :], gx[:, hf, :], 0.5, None, ALU.is_gt, ALU.add, accum_out=nout[:, hf:hf + 1])
            link(ins)
            V.scalar_tensor_tensor(out=gv[:, :, :], in0=gx[:, :, :], scalar=4096.0, in1=gv[:, :, :],
                                   op0=ALU.mult, op1=ALU.add).then_inc(g_ready, 1)

            split(3)
            ln_scale(2)
            split(4)
            dve.wait_ge(full("cols"), uses["cols"][1])
            acc = bank[uses["cols"][0]]
            V.tensor_copy(bcol[:, :, :], acc[:, 0:NSTEP].unsqueeze(2).to_broadcast([P, NSTEP, 2]))
            V.tensor_copy(vcol[:, :, :], acc[:, NSTEP:2 * NSTEP].unsqueeze(2).to_broadcast([P, NSTEP, 2])
                          ).then_inc(read("cols"), 1)
            stored(dve, "cols")
            dve.wait_ge(full("out"), uses["out"][1])
            V.tensor_scalar(fl[0:1, 1:2], bank[uses["out"][0]][0:1, 0:1], float(NSTEP * P - E), None, ALU.is_equal
                            ).then_inc(read("out"), 1)
            stored(dve, "out")
            V.tensor_copy(flag[:, :], fl[0:1, 1:2]).then_inc(flag_ready, 1)
            one_hots()
            landed(dve, "vec")
            V.tensor_copy(vec[:, :], bank[uses["vec"][0]][:, 0:20]).then_inc(read("vec"), 1)
            landed(dve, "proj")
            V.tensor_copy(pT[:, :], bank[uses["proj"][0]][:, 0:M]).then_inc(read("proj"), 1)
            split(5)
            split(6)
            one_hots()
            bn_piece(0)
            split(7)
            split(8)
            bn_piece(1)
            split(9)
            one_hots()
            bn_piece(2)
            for f in range(FT):
                ins = V.bn_aggr(mv1[:, f, :], st1[:, f, :, :].rearrange("p c s -> p (c s)"))
            link(ins)
            link(V.tensor_scalar(bw[:, 0, :], mv1[:, :, 1], EPS, None, ALU.add))
            V.tensor_scalar(bw[:, 4, :], mv1[:, :, 1], EPS, None, ALU.add).then_inc(bn_var, 1)
            one_hots()

            for t in range(AT):
                one_hots()

            dve.wait_ge(bn_std, 1)
            rstd(bw[:, 0, :], bw[:, 1, :], bw[:, 2, :], bw[:, 3, :])
            link(V.tensor_tensor(s1[:, :], vec[:, 4 * V_G1:4 * V_G1 + 4], bw[:, 2, :], ALU.mult))
            link(V.tensor_tensor(bw[:, 3, :], mv1[:, :, 0], s1[:, :], ALU.mult))
            link(V.tensor_tensor(t1[:, :], vec[:, 4 * V_B1:4 * V_B1 + 4], bw[:, 3, :], ALU.subtract))

            acc = landed(dve, "diag")
            V.tensor_copy(diag[:, :, :, :].rearrange("p j t h -> p (j t h)"), acc[:, 0:32]).then_inc(read("diag"), 1)
            stored(dve, "diag")
            for h in range(HEADS):
                stored(dve, ("uk", h))
                ins = V.tensor_reduce(mxk[:, :, h], kf[:, :, h, :], AX_X, ALU.max)
                if h == 1:
                    one_hots()
            link(ins)
            V.tensor_tensor(mxk1[:, :], mxk[:, 0, :], mxk[:, 1, :], ALU.max).then_inc(kmax_part, 1)
            def source_sum(c):
                c0, cn = CHUNKS[c]
                dve.wait_ge(group_stored, -(-(c0 + cn) // (GW * W)))
                if c > 1:
                    landed(dve, ("agg", c - 1, FT))
                t = asum[:, 0:4 * cn].rearrange("p (s n) -> p s n", s=4)
                link(V.tensor_tensor(t, A16[:, 0:4, c0:c0 + cn], A16[:, 4:8, c0:c0 + cn], ALU.add))
                link(V.tensor_tensor(t[:, 0:2, :], t[:, 0:2, :], t[:, 2:4, :], ALU.add))
                link(V.tensor_tensor(t[:, 0:2, :], t[:, 0:2, :], A16[:, 8:10, c0:c0 + cn], ALU.add))
                V.tensor_tensor(t[:, 0, :], t[:, 0, :], t[:, 1, :], ALU.add).then_inc(asum_ready, 1)

            def in_degrees(c):
                c0, cn = CHUNKS[c]
                acc = landed(dve, ("agg", c, FT))
                link(V.tensor_scalar(rdeg[:, c0:c0 + cn], acc[:, 0:cn], HSCALE, None, ALU.max))
                V.tensor_scalar(has_in[:, 0:cn], acc[:, 0:cn], 1.0, None, ALU.min).then_inc(read(("agg", c, FT)), 1)
                link(V.reciprocal(rdeg[:, c0:c0 + cn], rdeg[:, c0:c0 + cn]))

            def mean(c, f):
                c0, cn = CHUNKS[c]
                acc = landed(dve, ("agg", c, f))
                V.scalar_tensor_tensor(out=aggT[:, f, c0:c0 + cn], in0=acc[:, 0:cn], scalar=s1[:, f:f + 1],
                                       in1=rdeg[:, c0:c0 + cn], op0=ALU.mult, op1=ALU.mult).then_inc(read(("agg", c, f)), 1)
                stored(dve, ("agg", c, f))
                V.scalar_tensor_tensor(out=aggT[:, f, c0:c0 + cn], in0=has_in[:, 0:cn], scalar=t1[:, f:f + 1],
                                       in1=aggT[:, f, c0:c0 + cn], op0=ALU.mult, op1=ALU.add).then_inc(mean_ready, 1)

            def q_bias(h):
                acc = landed(dve, ("uq", h))
                link(V.tensor_reduce(mxq[:, :, h], acc[:, :].rearrange("p (t m) -> p t m", t=AT), AX_X, ALU.max))
                V.scalar_tensor_tensor(out=qb[:, :, h], in0=mxq[:, :, h], scalar=-1.0,
                                       in1=diag[:, 0, :, h], op0=ALU.mult, op1=ALU.subtract).then_inc(qb_ready, 1)

            def q_feat(h):
                acc = landed(dve, ("qfT", h))
                if h == 0:
                    landed(dve, ("k", 1))
                V.tensor_scalar(qfT[:, :, h, :], acc[:, :].rearrange("p (m n) -> p m n", m=2), PHI_SCALE, KEPS,
                                ALU.mult, ALU.add).then_inc(read(("qfT", h)), 1)

            q_bias(0)
            q_bias(1)
            acc = landed(dve, "kmaxT")
            V.tensor_reduce(mk8[:, :], acc[0:HEADS, 0:P], AX_X, ALU.max).then_inc(read("kmaxT"), 1)
            stored(dve, "kmaxT")
            V.tensor_scalar(dg8[:, :], ident[0:HEADS, 0:HEADS], mk8[:, 0:1], None, ALU.mult).then_inc(kmax_diag, 1)

            acc = landed(dve, "kmax")
            for t in range(AT):
                ins = V.scalar_tensor_tensor(out=kb[:, t, :], in0=acc[:, 0:HEADS], scalar=-1.0, in1=diag[:, 1, t, :],
                                             op0=ALU.mult, op1=ALU.subtract)
            ins.then_inc(read("kmax"), 1)
            one_hots()
            q_bias(2)
            q_bias(3)
            one_hots()
            for hp in range(4):
                q_feat(2 * hp)
                if hp < 2:
                    q_bias(2 * hp + 4)
                    q_bias(2 * hp + 5)
                else:
                    t = hp - 2
                    dve.wait_ge(k_exp, HEADS * (t + 1))
                    V.tensor_scalar(kf[:, t, :, :], kf[:, t, :, :], PHI_SCALE, KEPS, ALU.mult, ALU.add).then_inc(kf_ready, 1)
                if hp < 3:
                    one_hots()
            for i in range(4):
                m, half = divmod(i, 2)
                acc = landed(dve, ("kv", i))
                V.tensor_copy(kv[:, m, 4 * half:4 * half + 4, :], acc[:, 0:4 * (DH + 1)].rearrange("p (h d) -> p h d", h=4)
                              ).then_inc(read(("kv", i)), 1)
                one_hots()
            for i in range(4):
                t, half = divmod(i, 2)
                acc = landed(dve, ("attn", i))
                a = acc[:, 0:4 * (DH + 1)].rearrange("p (h d) -> p h d", h=4)
                link(V.tensor_scalar(zz[:, i, :], a[:, :, DH], KEPS, None, ALU.add))
                link(V.reciprocal(zr[:, i, :], zz[:, i, :]))
                V.tensor_tensor(attn[:, t, half * 256:(half + 1) * 256].rearrange("p (h d) -> p h d", h=4), a[:, :, 0:DH],
                                zr[:, i, :].unsqueeze(2).to_broadcast([P, 4, DH]), ALU.mult).then_inc(read(("attn", i)), 1)
                if i % 2:
                    one_hots()
            in_degrees(0)
            mean(0, 0)
            one_hots()
            for i in range(2):
                acc = landed(dve, ("attnT", i))
                V.tensor_copy(attnT[:, 2 * i:2 * i + 2, :], acc[:, :].rearrange("p (t n) -> p t n", t=2)
                              ).then_inc(read(("attnT", i)), 1)
            one_hots()
            mean(0, 1)
            one_hots()
            for i in range(2):
                acc = landed(dve, ("ha", i))
                V.tensor_copy(haT[:, 2 * i:2 * i + 2, :], acc[:, :].rearrange("p (t n) -> p t n", t=2)
                              ).then_inc(read(("ha", i)), 1)
                stored(dve, ("ha", i))
                if i == 0:
                    source_sum(1)
            V.tensor_tensor(hT[:, :, 0:NA], hT[:, :, 0:NA], haT[:, :, :], ALU.add).then_inc(hTa_ready, 1)

            dve.wait_ge(hTa_ready, 1)
            one_hots()
            mean(0, 2)
            one_hots()
            mean(0, 3)
            in_degrees(1)
            one_hots()
            for f in range(FT):
                mean(1, f)
                if f == 0:
                    one_hots()
                if f == 2:
                    source_sum(2)
            covered = dve.value_load(flag[0:1, 0:1], min_val=0, max_val=1)
            links = step[0]
            with dve.If(covered == 1):
                V.memset(fl[0:1, 0:1], 0.0).then_inc(sums_final, 1)
                in_degrees(2)
                for f in range(FT):
                    mean(2, f)
            with dve.Else():
                step[0] = links
                in_degrees(2)
                for f in range(FT):
                    mean(2, f)
                nprep = [0]

                def prep(ins):
                    nprep[0] += 1
                    ins.then_inc(s_prep, 1)
                    dve.wait_ge(s_prep, nprep[0])

                dve.wait_ge(src_in, 16)
                prep(V.tensor_scalar(si[:, 0, :], esrc[:, :], 7, None, ALU.arith_shift_right))
                prep(V.tensor_scalar(si[:, 1, :], esrc[:, :], P - 1, None, ALU.bitwise_and))
                prep(V.tensor_copy(sa[:, :], si[:, 0, :]))
                prep(V.tensor_copy(sbb[:, :], si[:, 1, :]))
                prep(V.tensor_copy(sd[:, :], edst[:, :]))
                prep(V.memset(wbase[:, :], 0.0))
                V.memset(fl[0:1, 0:1], 0.0).then_inc(s_used, 1)
                with dve.Fori(0, NWS) as w:
                    seq = [0]

                    def chain(ins):
                        seq[0] += 1
                        ins.then_inc(s_link, 1)
                        dve.wait_ge(s_link, w * SLOW_LINKS + seq[0])

                    chain(V.tensor_scalar(sx[:, :], sd[:, :], wbase[:, 0:1], None, ALU.subtract))
                    chain(V.scalar_tensor_tensor(out=sv[:, :], in0=sa[:, :], scalar=float(WS), in1=sx[:, :],
                                                 op0=ALU.mult, op1=ALU.add))
                    chain(V.tensor_scalar(sw[:, :], sx[:, :], 0.0, None, ALU.is_lt))
                    chain(V.scalar_tensor_tensor(out=sx[:, :], in0=sx[:, :], scalar=WS - 0.5, in1=sw[:, :],
                                                 op0=ALU.is_gt, op1=ALU.add))
                    chain(V.tensor_scalar(sx[:, :], sx[:, :], 4096.0, None, ALU.mult))
                    chain(V.tensor_tensor(sv[:, :], sv[:, :], sx[:, :], ALU.add))
                    seq[0] += 1
                    V.tensor_scalar(wbase[:, :], wbase[:, :], float(WS), None, ALU.add).then_inc(s_link, 1)
                    with dve.Fori(0, EJ // 8) as gg:
                        dve.wait_ge(s_used, w * (EJ // 8) + gg + 1)
                        for s in range(8):
                            V.tensor_scalar(sohb[:, s, :], iota16[0:EP, 0:P], sbb[:, ds(8 * gg + s, 1)], None, ALU.is_equal)
                            last = V.tensor_scalar(sohv[:, s, :], iota16[0:EP, 0:NT * WS], sv[:, ds(8 * gg + s, 1)], None, ALU.is_equal)
                        last.then_inc(s_oh, 1)
                    dve.wait_ge(s_count, w + 1)
                    cnt = bank[0][:, 0:NT * WS].rearrange("p (a d) -> p a d", a=NT)
                    chain(V.tensor_copy(aw[:, 0, :, :], cnt))
                    V.tensor_tensor(aw[:, 1, :, :], cnt, aw[:, 0, :, :], ALU.subtract).then_inc(s_aw, 1)
                    dve.wait_ge(s_agg, w + 1)
                    for f in range(FT):
                        V.tensor_copy(aggT[:, f, ds(WS * w, WS)], bank[2 + f][:, 0:WS])
                    V.tensor_copy(deg[:, ds(WS * w, WS)], bank[6][:, 0:WS]).then_inc(s_read, 1)
                prep(V.memset(fl[0:1, 0:1], 0.0))
                prep(V.tensor_scalar(rdeg, deg, HSCALE, None, ALU.max))
                prep(V.reciprocal(rdeg, rdeg))
                for c0, cn in CHUNKS:
                    prep(V.tensor_scalar(has_in[:, 0:cn], deg[:, c0:c0 + cn], 1.0, None, ALU.min))
                    for f in range(FT):
                        prep(V.scalar_tensor_tensor(out=aggT[:, f, c0:c0 + cn], in0=aggT[:, f, c0:c0 + cn], scalar=s1[:, f:f + 1],
                                                    in1=rdeg[:, c0:c0 + cn], op0=ALU.mult, op1=ALU.mult))
                        prep(V.scalar_tensor_tensor(out=aggT[:, f, c0:c0 + cn], in0=has_in[:, 0:cn], scalar=t1[:, f:f + 1],
                                                    in1=aggT[:, f, c0:c0 + cn], op0=ALU.mult, op1=ALU.add))
                V.memset(fl[0:1, 0:1], 0.0).then_inc(sums_final, 1)

            ny = [0]

            def add_y(c):
                c0, cn = CHUNKS[c]
                for f in range(FT):
                    stored(dve, ("conv", c, f))
                    own = max(0, min(NA - c0, cn))
                    if own:
                        ins = V.tensor_tensor(yT[:, f, c0:c0 + own], yT[:, f, c0:c0 + own], hT[:, f, c0:c0 + own], ALU.add)
                    ins = V.scalar_tensor_tensor(out=yT[:, f, c0 + own:c0 + cn], in0=hT[:, f, c0 + own:c0 + cn],
                                                 scalar=haT[:, f, NA - 1:NA], in1=yT[:, f, c0 + own:c0 + cn],
                                                 op0=ALU.add, op1=ALU.add)
                    ny[0] += 1
                    ins.then_inc(y_ready, 1)
                    dve.wait_ge(y_ready, ny[0])
                    ins = V.bn_stats(st1[:, f, c, :], yT[:, f, c0:c0 + cn])
                return ins

            add_y(0)
            add_y(1)
            link(add_y(2))
            for f in range(FT):
                ins = V.bn_aggr(mv1[:, f, :], st1[:, f, :, :].rearrange("p c s -> p (c s)"))
            link(ins)
            V.tensor_scalar(bw[:, 0, :], mv1[:, :, 1], EPS, None, ALU.add).then_inc(bn_var, 1)
            dve.wait_ge(bn_std, 2)
            rstd(bw[:, 0, :], bw[:, 1, :], bw[:, 2, :], bw[:, 3, :])
            link(V.tensor_tensor(s2[:, :], vec[:, 4 * V_G2:4 * V_G2 + 4], bw[:, 2, :], ALU.mult))
            link(V.tensor_tensor(bw[:, 3, :], mv1[:, :, 0], s2[:, :], ALU.mult))
            V.tensor_tensor(t2[:, :], vec[:, 4 * V_B2:4 * V_B2 + 4], bw[:, 3, :], ALU.subtract).then_inc(st2_ready, 1)
            dve.wait_ge(st2_ready, 1)

            def z(c):
                for cc, f in Z_DVE:
                    if cc == c:
                        c0, cn = ZC[c]
                        V.tensor_scalar(yT[:, f, c0:c0 + cn], yT[:, f, c0:c0 + cn], s2[:, f:f + 1], t2[:, f:f + 1],
                                        ALU.mult, ALU.add).then_inc(z_dve, 1)

            def finish(i):
                n = P if i < NT - 1 else LAST
                acc = landed(dve, ("zT", i))
                V.tensor_tensor(xs[0:n, i, :], acc[0:n, :], xs[0:n, i, :], ALU.add).then_inc(o_ready, 1)

            z(0)
            z(1)
            finish(0)
            finish(1)
            z(2)
            finish(2)
            finish(3)
            z(3)
            for i in range(4, NT):
                finish(i)


_INS = ['x', 'src', 'dst', 'L0_gnn_norm1_g', 'L0_gnn_norm1_b', 'L0_gnn_norm2_g', 'L0_gnn_norm2_b', 'L0_gnn_W_conv',
        'L0_gnn_b_conv', 'L0_gnn_Wq', 'L0_gnn_Wk', 'L0_gnn_Wv', 'L0_gnn_Wo', 'L0_gnn_proj']


def kernel(**inputs):
    import numpy as _np
    import concourse.bacc as _bacc
    from concourse import mybir as _mybir
    from concourse.bass_utils import run_bass_kernel_spmd as _run

    nc = _bacc.Bacc("TRN2", target_bir_lowering=False, num_devices=1)
    arrays, args = {}, []
    for name in _INS:
        a = _np.ascontiguousarray(inputs[name])
        arrays[f"in_{name}"] = a
        args.append(nc.dram_tensor(f"in_{name}", a.shape, _mybir.dt.from_np(a.dtype), kind="ExternalInput").ap())
    out = nc.dram_tensor("out", (N, D), F32, kind="ExternalOutput").ap()
    gnn_kernel(nc, *args, out)
    r = _run(nc, [arrays], core_ids=[0])
    return r.results[0]["out"]
```
